# Optimizing a Trainium2 kernel written in Bass

```python
import numpy as np
import jax
import jax.numpy as jnp

def _softmax(x, axis=-1):
    return jax.nn.softmax(x, axis=axis)
def _gelu(x):
    return jax.nn.gelu(x, approximate=True)
def _silu(x):
    return jax.nn.silu(x)
def _sigmoid(x):
    return jax.nn.sigmoid(x)
def _layernorm(x, axis=-1, eps=1e-5):
    m = jnp.mean(x, axis=axis, keepdims=True)
    v = jnp.var(x, axis=axis, keepdims=True)
    return (x - m) / jnp.sqrt(v + eps)
def _scatter_add(tgt, idx, src, axis=0):
    return tgt.at[idx].add(src)
def _segment_sum(src, seg, n):
    return jax.ops.segment_sum(src, seg, n)

kernel_name = 'mk_adj_preln_d2_adj_128_79e8d4'

def setup_inputs(seed: int = 0):
    np.random.seed(seed)
    _w = jnp.asarray
    def _rec_inputs():
        import jax
        import jax.numpy as jnp
        _gk = jax.random.key(seed)
        x = -0.0005207 + 1.001 * jax.random.normal(jax.random.fold_in(_gk, 1), (8192, 128), jnp.float32)
        _w = (1.0 + jnp.arange(8192, dtype=jnp.float32)) ** -0.5
        _w = _w / _w.mean()
        _pij = jnp.clip(0.00390625 * _w[:, None] * _w[None, :], 0.0, 1.0)
        _a = jax.random.uniform(jax.random.fold_in(_gk, 2), (8192, 8192)) < _pij
        _a = jnp.logical_or(_a, jnp.eye(8192, dtype=bool))
        _af = _a.astype(jnp.float32)
        _af = _af * jax.random.uniform(jax.random.fold_in(_gk, 3), (8192, 8192), jnp.float32, 0.05, 1)
        adj = _af
        return x, adj
    x, adj = _rec_inputs()
    def _L0_gnn_setup():
        import jax, jax.numpy as jnp
        import numpy as np
        N = 16384
        IN_DIM = 128
        OUT_DIM = 128

        def _message(X, A, W):
            deg = jnp.sum(A, axis=1, keepdims=True)
            A_norm = A / jnp.where(deg > 0, deg, 1.0)
            return A_norm @ X @ W
        key = jax.random.key(seed)
        k1, k2, k3, k4 = jax.random.split(key, 4)
        X = jax.random.normal(k1, (N, IN_DIM), dtype=jnp.float32)
        A = jax.random.uniform(k2, (N, N), dtype=jnp.float32)
        W_in = jax.random.normal(k3, (IN_DIM, OUT_DIM), dtype=jnp.float32) / np.sqrt(IN_DIM)
        W_out = jax.random.normal(k4, (IN_DIM, OUT_DIM), dtype=jnp.float32) / np.sqrt(IN_DIM)
        return {'X': X, 'A': A, 'W_in': W_in, 'W_out': W_out}
    _L0_gnn_all = _L0_gnn_setup()
    _L0_gnn_in = {k: v for k, v in _L0_gnn_all.items() if k in ('W_in', 'W_out', )}
    del _L0_gnn_all

    def _L1_gnn_setup():
        import jax, jax.numpy as jnp
        import numpy as np
        NEG = -9000000000000000.0
        ALPHA = 0.2
        key = jax.random.key(seed)
        k1, k2, k3, k4, k5 = jax.random.split(key, 5)
        N, F_in, F_out = (8192, 128, 128)
        x = jax.random.normal(k1, (N, F_in), dtype=jnp.float32)
        adj = jax.random.randint(k2, (N, N), 0, 2).astype(jnp.float32)
        W = jax.random.normal(k3, (F_in, F_out), dtype=jnp.float32) * (1.0 / np.sqrt(F_in))
        a1 = jax.random.normal(k4, (F_out,), dtype=jnp.float32) * (1.0 / np.sqrt(2 * F_out))
        a2 = jax.random.normal(k5, (F_out,), dtype=jnp.float32) * (1.0 / np.sqrt(2 * F_out))
        a_bias = jnp.zeros((1,), dtype=jnp.float32)
        return {'x': x, 'adj': adj, 'W': W, 'a1': a1, 'a2': a2, 'a_bias': a_bias}
    _L1_gnn_all = _L1_gnn_setup()
    _L1_gnn_in = {k: v for k, v in _L1_gnn_all.items() if k in ('W', 'a1', 'a2', 'a_bias', )}
    del _L1_gnn_all

    return {
        "x": x,
        "adj": adj,
        "L0_gnn_W_in": _L0_gnn_in["W_in"],
        "L0_gnn_W_out": _L0_gnn_in["W_out"],
        "L1_gnn_W": _L1_gnn_in["W"],
        "L1_gnn_a1": _L1_gnn_in["a1"],
        "L1_gnn_a2": _L1_gnn_in["a2"],
        "L1_gnn_a_bias": _L1_gnn_in["a_bias"],
    }

def reference(x, adj, L0_gnn_W_in, L0_gnn_W_out, L1_gnn_W, L1_gnn_a1, L1_gnn_a2, L1_gnn_a_bias):
    import jax
    import jax.numpy as jnp
    def _L0_gnn_ref(X, A, W_in, W_out):
        import jax, jax.numpy as jnp
        import numpy as np
        N = 16384
        IN_DIM = 128
        OUT_DIM = 128

        def _message(X, A, W):
            deg = jnp.sum(A, axis=1, keepdims=True)
            A_norm = A / jnp.where(deg > 0, deg, 1.0)
            return A_norm @ X @ W
        X_in = _message(X, A, W_in)
        X_out = _message(X, A.T, W_out)
        return X_in + X_out

    def _L1_gnn_ref(x, adj, W, a1, a2, a_bias):
        import jax, jax.numpy as jnp
        import numpy as np
        NEG = -9000000000000000.0
        ALPHA = 0.2
        h = x @ W
        s1 = h @ a1
        s2 = h @ a2
        e = jax.nn.leaky_relu(s1[:, None] + s2[None, :] + a_bias[0], negative_slope=ALPHA)
        e = jnp.where(adj > 0, e, NEG)
        attention = jax.nn.softmax(e, axis=1)
        return attention @ h

    h = jnp.maximum(_layernorm(x, axis=-1), 0.0)
    x = x + _L0_gnn_ref(h, adj, L0_gnn_W_in, L0_gnn_W_out)
    h = jnp.maximum(_layernorm(x, axis=-1), 0.0)
    x = x + _L1_gnn_ref(h, adj, L1_gnn_W, L1_gnn_a1, L1_gnn_a2, L1_gnn_a_bias)
    return x


_drawn_inputs = setup_inputs


def setup_inputs(seed=0):
    import zlib

    import numpy as np

    out = dict(_drawn_inputs(seed))
    spreads = {}
    factors = {}
    for name, (base, spread) in spreads.items():
        noise = np.random.default_rng([zlib.crc32(name.encode()), seed]).standard_normal(out[name].shape)
        drawn = base * np.exp(spread * noise) if base else spread * noise
        out[name] = jnp.asarray(drawn.astype(out[name].dtype))
    for name, factor in factors.items():
        out[name] = (out[name] * factor).astype(out[name].dtype)
    return out
```

```python
from contextlib import ExitStack

import concourse.bass as bass
from concourse import mybir

F32 = mybir.dt.float32
F32R = mybir.dt.float32r
U8 = mybir.dt.uint8
ALU = mybir.AluOpType
ACT = mybir.ActivationFunctionType
AX_X = mybir.AxisListType.X

P = 128
EPS = 1e-5
SLOPE = 0.2
CAP = float(2.0 ** 90)


def graph_layers(nc, x, adj, w_in, w_out, w_att, a1, a2, a_bias, out):
    N, D = x.shape
    assert D == P
    NT = N // P
    IT = 4
    ROWS = IT * P
    IB = N // ROWS
    JT = 8
    COLS = JT * P
    CB = N // COLS
    STEPS = CB * IB
    SUB = JT // 2
    LNT = 8
    assert SUB == IT and CB * LNT == NT and IB == 2 * CB

    x_rows = x.rearrange("(c t p) d -> c p t d", p=P, t=LNT)
    adj_v = adj.rearrange("(b t p) (c w) -> b c p t w", t=IT, p=P, w=COLS)
    mask_dram = nc.dram_tensor("mask_scratch", (IB, P, NT, ROWS), U8, kind="Internal").ap()
    out_rows = out.rearrange("(b t p) d -> b p t d", t=IT, p=P)

    with ExitStack() as whole:
        def keep(name, shape, dt=F32):
            return whole.enter_context(nc.sbuf_tensor(name, shape, dt))

        in_sum = keep("in_sum", [P, N])
        out_sum = keep("out_sum", [P, N])
        row_parts = keep("row_parts", [P, NT, CB])
        col_parts = keep("col_parts", [P, NT, IB])
        ident = keep("ident", [P, P])
        eps = keep("eps", [P, 1])
        stats = keep("stats", [P, 2, LNT, 6])
        moments = keep("moments", [P, 2, LNT, 2])
        std = keep("std", [P, 2, LNT])
        rstd0 = keep("rstd0", [P, 2, LNT])
        newton = keep("newton", [P, 2, LNT])
        rstd = keep("rstd", [P, 2, LNT])
        shift = keep("shift", [P, 2, LNT])

        waits_done = whole.enter_context(nc.semaphore("waits_done"))

        def wait_alone(eng, sem, value):
            eng.wait_ge(sem, value)
            eng.sem_inc(waits_done, 1)

        STATS_CHAIN, FACTORS_CHAIN = 1, 5

        def norm_stats(dve, T, q, row_tile, chain, before, stats_ready):
            for t in range(T):
                ins = dve.bn_stats(stats[:, q, t, :], row_tile(t))
            ins.then_inc(chain, 1)
            wait_alone(dve, chain, before + 1)
            for t in range(T):
                ins = dve.bn_aggr(moments[:, q, t, :], stats[:, q, t, :])
            ins.then_inc(stats_ready, 1)

        def norm_factors(dve, T, q, chain, before, factors_ready):
            r0, nt, r = rstd0[:, q, 0:T], newton[:, q, 0:T], rstd[:, q, 0:T]
            dve.reciprocal(r0, std[:, q, 0:T]).then_inc(chain, 1)
            dve.wait_ge(chain, before + 1)
            dve.tensor_tensor(nt, r0, r0, ALU.mult).then_inc(chain, 1)
            dve.wait_ge(chain, before + 2)
            dve.scalar_tensor_tensor(out=nt, in0=moments[:, q, 0:T, 1], scalar=EPS,
                                     in1=nt, op0=ALU.add, op1=ALU.mult).then_inc(chain, 1)
            dve.wait_ge(chain, before + 3)
            dve.tensor_scalar(nt, nt, -0.5, 1.5, ALU.mult, ALU.add).then_inc(chain, 1)
            dve.wait_ge(chain, before + 4)
            dve.tensor_tensor(r, r0, nt, ALU.mult).then_inc(chain, 1)
            dve.wait_ge(chain, before + 5)
            dve.scalar_tensor_tensor(out=shift[:, q, 0:T], in0=moments[:, q, 0:T, 0], scalar=-1.0,
                                     in1=r, op0=ALU.mult, op1=ALU.mult).then_inc(factors_ready, 1)

        with ExitStack() as ctx:
            def sb(name, shape, dt=F32):
                return ctx.enter_context(nc.sbuf_tensor(name, shape, dt))

            def sem(name):
                return ctx.enter_context(nc.semaphore(name))

            h0 = sb("h0", [P, N])
            a_tile = sb("a_tile", [P, 2, IT, COLS])
            lie_hi = sb("lie_hi", [P, 2, COLS], F32R)
            lie_lo = sb("lie_lo", [P, 2, COLS], F32R)
            turn_hi = sb("turn_hi", [P, 2, 2, ROWS], F32R)
            turn_lo = sb("turn_lo", [P, 2, 2, ROWS], F32R)
            mask = sb("mask", [P, 2, JT, ROWS], U8)
            rowh_hi = sb("rowh_hi", [P, 2, ROWS], F32R)
            rowh_lo = sb("rowh_lo", [P, 2, ROWS], F32R)
            colh_hi = sb("colh_hi", [P, COLS], F32R)
            colh_lo = sb("colh_lo", [P, COLS], F32R)
            turned = ctx.enter_context(nc.psum_tensor("turned", [P, 2, 2, ROWS], F32))
            acc_in = ctx.enter_context(nc.psum_tensor("acc_in", [P, 2, ROWS], F32))
            acc_out = ctx.enter_context(nc.psum_tensor("acc_out", [P, 2, COLS // 2], F32))

            TURN_SLOTS = LIE_SLOTS = ACC_SLOTS = 2
            LIE_CREDIT = 2 * SUB
            MASK_CREDIT = 16
            NORM_STATS, NORM_ROOT, NORM_FACTORS = (0, 1), (0, 3), (0, 4)
            NORM_TILES = {(0, 5): (0, 1), (0, 6): (2, 3), (0, 7): (4, 5), (1, 0): (6, 7)}
            ORDER = [(True, 0), (True, 1), (False, 0), (False, 1), (True, 2), (False, 2), (True, 3), (False, 3)]
            x_loaded = [sem(f"x_loaded{c}") for c in range(CB)]
            a_loaded = [sem(f"a_loaded{i}") for i in range(2)]
            mask_stored = [sem(f"mask_stored{i}") for i in range(2)]
            ident_zero = sem("ident_zero")
            ident_ready = sem("ident_ready")
            eps_ready = sem("eps_ready")
            sum_cleared = sem("sum_cleared")
            ln_chain = sem("ln_chain")
            stats_ready = sem("stats_ready")
            sqrt_done = sem("sqrt_done")
            factors_ready = sem("factors_ready")
            h0_ready = sem("h0_ready")
            rowh_hi_done = sem("rowh_hi_done")
            rowh_ready = sem("rowh_ready")
            colh_hi_done = sem("colh_hi_done")
            colh_ready = sem("colh_ready")
            turned_done = sem("turned_done")
            turn_hi_done = sem("turn_hi_done")
            turn_ready = sem("turn_ready")
            turn_used = sem("turn_used")
            mask_done = sem("mask_done")
            lie_hi_done = sem("lie_hi_done")
            lie_ready = sem("lie_ready")
            lie_used = sem("lie_used")
            in_added = sem("in_added")
            out_saved = sem("out_saved")

            block = ctx.enter_context(nc.Block("layer0"))

            @block.sync
            def _(sp):
                def load(b, c, par):
                    sp.dma_start(a_tile[:, par, :, :], adj_v[b, c]).then_inc(a_loaded[par], 16)

                def store_mask(n, b, c, par):
                    wait_alone(sp, mask_done, TURN_SLOTS + SUB * (n + 1))
                    sp.dma_start(mask_dram[b, :, bass.ds(c * JT, JT), :], mask[:, par, :, :]) \
                        .then_inc(mask_stored[par], 16)

                load(0, 0, 0)
                load(1, 0, 1)
                with sp.Fori(1, STEPS // 2) as g:
                    for par in range(2):
                        n = 2 * g + par
                        sp.wait_ge(turned_done, SUB * (n - 1))
                        wait_alone(sp, lie_ready, SUB * (n - 1))
                        load(n & (IB - 1), n // IB, par)
                        store_mask(n - 2, (n - 2) & (IB - 1), (n - 2) // IB, par)
                for par in range(2):
                    store_mask(STEPS - 2 + par, IB - 2 + par, CB - 1, par)
                for par in range(2):
                    sp.wait_ge(mask_stored[par], MASK_CREDIT + 16 * (STEPS // 2))

            @block.tensor
            def _(pe):
                def turn(n, u, par):
                    m = SUB * n + u
                    pe.wait_ge(turn_ready, m + 1)
                    for k in range(2):
                        for t in range(IT):
                            ins = pe.transpose(turned[:, u % 2, k, bass.ts(t, P)],
                                               a_tile[:, par, t, bass.ts(2 * u + k, P)], ident[:, :])
                    ins.then_inc(turned_done, 1)

                def lying_product(n, u, par, first):
                    pe.wait_ge(lie_ready, SUB * n + u + 1)
                    hi, lo = (h[:, par, bass.ts(u, P)] for h in (rowh_hi, rowh_lo))
                    s = u % 2
                    for i, (h, a) in enumerate(((hi, lie_hi), (hi, lie_lo), (lo, lie_hi))):
                        for half in range(2):
                            ins = pe.matmul(acc_out[:, half, :], h, a[:, s, bass.ts(half, COLS // 2)],
                                            start=(first and u == 0 and i == 0), stop=(i == 2),
                                            skip_group_check=True)
                    ins.then_inc(lie_used, 1)

                def turned_product(n, u, par, c):
                    pe.wait_ge(turn_ready, TURN_SLOTS + SUB * n + u + 1)
                    pe.wait_ge(colh_ready, SUB * c + u + 1)
                    s = u % 2
                    for k in range(2):
                        hi, lo = (h[:, bass.ts(2 * u + k, P)] for h in (colh_hi, colh_lo))
                        for i, (h, a) in enumerate(((hi, turn_hi), (hi, turn_lo), (lo, turn_hi))):
                            ins = pe.matmul(acc_in[:, par, :], h, a[:, s, k, :],
                                            start=(u == 0 and k == 0 and i == 0),
                                            stop=(u == SUB - 1 and k == 1 and i == 2))
                    ins.then_inc(turn_used, 1)

                def pair(c, p, first):
                    for par in range(2):
                        n = IB * c + 2 * p + par
                        new = first and par == 0
                        pe.wait_ge(a_loaded[par], 16 * ((IB // 2) * c + p + 1))
                        turn(n, 0, par)
                        pe.wait_ge(rowh_ready, n + 1)
                        if new:
                            pe.wait_ge(out_saved, c + 1)
                        lying_product(n, 0, par, new)
                        turn(n, 1, par)
                        lying_product(n, 1, par, False)
                        pe.wait_ge(in_added, n + 1)
                        turned_product(n, 0, par, c)
                        turn(n, 2, par)
                        turned_product(n, 1, par, c)
                        turn(n, 3, par)
                        for u in range(2, SUB):
                            lying_product(n, u, par, False)
                            turned_product(n, u, par, c)

                pe.wait_ge(ident_ready, 1)
                with pe.Fori(0, CB) as c:
                    pair(c, 0, True)
                    with pe.Fori(1, IB // 2) as p:
                        pair(c, p, False)

            @block.scalar
            def _(act):
                for c in range(CB):
                    act.dma_start(out_sum[:, bass.ts(c, LNT * P)].rearrange("p (t d) -> p t d", d=P),
                                  x_rows[c]).then_inc(x_loaded[c], 16)

                def root(c):
                    act.wait_ge(stats_ready, c + 1)
                    nc.scalar.activation(std[:, 0, :], moments[:, 0, :, 1], ACT.Sqrt, bias=eps[:, 0:1]) \
                        .then_inc(sqrt_done, 1)

                def normalise(c, tiles):
                    act.wait_ge(factors_ready, c + 1)
                    for t in tiles:
                        at = bass.ds((c * LNT + t) * P, P)
                        ins = nc.scalar.activation(h0[:, at], out_sum[:, at], ACT.Relu,
                                                   bias=shift[:, 0, t:t + 1], scale=rstd[:, 0, t:t + 1])
                    if LNT - 1 in tiles:
                        ins.then_inc(h0_ready, 1)

                def pair(c, p, norm=None):
                    for par in range(2):
                        n = IB * c + 2 * p + par
                        b = 2 * p + par
                        act.wait_ge(a_loaded[par], 16 * ((IB // 2) * c + p + 1))
                        for item, (lying, u) in enumerate(ORDER):
                            if norm is not None and (par, item) == NORM_ROOT:
                                root(norm)
                            if norm is not None and (par, item) in NORM_TILES:
                                normalise(norm, NORM_TILES[par, item])
                            m = SUB * n + u
                            s = u % 2
                            if lying:
                                act.wait_ge(lie_used, m + LIE_CREDIT - LIE_SLOTS + 1)
                                nc.scalar.activation(lie_hi[:, s, :], a_tile[:, par, u, :], ACT.Copy,
                                                     accum_out=row_parts[:, b * IT + u, bass.ds(c, 1)]) \
                                    .then_inc(lie_hi_done, 1)
                                continue
                            act.wait_ge(turned_done, m + 1)
                            act.wait_ge(turn_used, m + 1)
                            act.wait_ge(mask_done, m + 1)
                            for k in range(2):
                                ins = nc.scalar.activation(
                                    turn_hi[:, s, k, :], turned[:, s, k, :], ACT.Copy,
                                    accum_out=col_parts[:, c * JT + 2 * u + k, bass.ds(b, 1)])
                            ins.then_inc(turn_hi_done, 1)

                def save_out(c):
                    act.wait_ge(lie_used, LIE_CREDIT + SUB * IB * (c + 1))
                    nc.scalar.copy(out_sum[:, bass.ts(c, COLS)], acc_out[:, :, :].rearrange("p a b -> p (a b)")) \
                        .then_inc(out_saved, 1)

                act.wait_ge(eps_ready, 1)
                root(0)
                normalise(0, range(LNT))
                with act.Fori(0, CB - 1) as p:
                    pair(0, p, p + 1)
                pair(0, CB - 1)
                save_out(0)
                with act.Fori(1, CB) as c:
                    with act.Fori(0, IB // 2) as p:
                        pair(c, p)
                    save_out(c)

            @block.vector
            def _(dve):
                dve.memset(eps[:, :], EPS).then_inc(eps_ready, 1)
                dve.sem_inc(turn_ready, TURN_SLOTS)
                dve.sem_inc(in_added, ACC_SLOTS)

                def layer_stats(c):
                    norm_stats(dve, LNT, 0, lambda t: out_sum[:, bass.ds((c * LNT + t) * P, P)],
                               ln_chain, (STATS_CHAIN + FACTORS_CHAIN) * c, stats_ready)

                def layer_factors(c):
                    dve.wait_ge(sqrt_done, c + 1)
                    norm_factors(dve, LNT, 0, ln_chain, (STATS_CHAIN + FACTORS_CHAIN) * c + STATS_CHAIN,
                                 factors_ready)

                def add_in(n, b, par):
                    dve.wait_ge(turn_used, TURN_SLOTS + SUB * (n + 1))
                    rows = in_sum[:, bass.ts(b, ROWS)]
                    dve.tensor_tensor(rows, acc_in[:, par, :], rows, ALU.add).then_inc(in_added, 1)

                def pair(c, p, norm=None, first=False):
                    for par in range(2):
                        n = IB * c + 2 * p + par
                        for item, (lying, u) in enumerate(ORDER):
                            if norm is not None and (par, item) == NORM_STATS:
                                layer_stats(norm)
                            if norm is not None and (par, item) == NORM_FACTORS:
                                dve.wait_ge(h0_ready, norm)
                                layer_factors(norm)
                            m = SUB * n + u
                            s = u % 2
                            if lying:
                                dve.wait_ge(lie_hi_done, m + 1)
                                dve.tensor_tensor(lie_lo[:, s, :], a_tile[:, par, u, :],
                                                  lie_hi[:, s, :].bitcast(F32), ALU.subtract).then_inc(lie_ready, 1)
                                continue
                            dve.wait_ge(turn_hi_done, m + 1)
                            dve.tensor_tensor(turn_lo[:, s, :, :].rearrange("p a b -> p (a b)"),
                                              turned[:, s, :, :].rearrange("p a b -> p (a b)"),
                                              turn_hi[:, s, :, :].rearrange("p a b -> p (a b)").bitcast(F32),
                                              ALU.subtract).then_inc(turn_ready, 1)
                            if u == 0:
                                dve.wait_ge(mask_stored[par], MASK_CREDIT + 16 * ((IB // 2) * c + p))
                            dve.tensor_scalar(mask[:, par, 2 * u:2 * u + 2, :].rearrange("p a b -> p (a b)"),
                                              turn_hi[:, s, :, :].rearrange("p a b -> p (a b)").bitcast(F32),
                                              0.0, None, ALU.is_gt).then_inc(mask_done, 1)
                            if u == 1 and not (first and par == 0):
                                add_in(n - 1, (2 * p + par + IB - 1) & (IB - 1), 1 - par)

                dve.wait_ge(x_loaded[0], 16)
                layer_stats(0)
                layer_factors(0)
                dve.wait_ge(sum_cleared, 1)
                dve.wait_ge(x_loaded[1], 16)
                pair(0, 0, norm=1, first=True)
                for c in range(2, CB):
                    dve.wait_ge(x_loaded[c], 16)
                with dve.Fori(1, CB - 1) as p:
                    pair(0, p, norm=p + 1)
                pair(0, CB - 1)
                with dve.Fori(1, CB) as c:
                    with dve.Fori(0, IB // 2) as p:
                        pair(c, p)
                add_in(STEPS - 1, IB - 1, 1)

            @block.gpsimd
            def _(pool):
                pool.sem_inc(turn_used, TURN_SLOTS)
                pool.sem_inc(lie_used, LIE_CREDIT)
                pool.sem_inc(mask_done, TURN_SLOTS)
                pool.sem_inc(out_saved, 1)
                for par in range(2):
                    pool.sem_inc(mask_stored[par], MASK_CREDIT)
                nc.gpsimd.memset(ident[:, :], 0.0).then_inc(ident_zero, 1)
                pool.wait_ge(ident_zero, 1)
                nc.gpsimd.affine_select(out=ident[:, :], in_=ident[:, :], compare_op=ALU.not_equal, fill=1.0,
                                        base=0, pattern=[[-1, P]], channel_multiplier=1).then_inc(ident_ready, 1)
                nc.gpsimd.memset(in_sum[:, :], 0.0).then_inc(sum_cleared, 1)

                def split_rows(n, b, par):
                    pool.wait_ge(lie_used, LIE_CREDIT + SUB * (n - 1))
                    h = h0[:, bass.ts(b, ROWS)]
                    nc.gpsimd.tensor_copy(rowh_hi[:, par, :], h).then_inc(rowh_hi_done, 1)
                    wait_alone(pool, rowh_hi_done, n + 1)
                    nc.gpsimd.tensor_tensor(rowh_lo[:, par, :], h, rowh_hi[:, par, :].bitcast(F32),
                                            ALU.subtract).then_inc(rowh_ready, 1)

                def split_columns(c):
                    pool.wait_ge(turn_used, TURN_SLOTS + SUB * IB * c)
                    pool.wait_ge(h0_ready, c + 1)
                    for u in range(SUB):
                        at = bass.ts(u, COLS // SUB)
                        h = h0[:, bass.ds(c * COLS + u * (COLS // SUB), COLS // SUB)]
                        nc.gpsimd.tensor_copy(colh_hi[:, at], h).then_inc(colh_hi_done, 1)
                        wait_alone(pool, colh_hi_done, SUB * c + u + 1)
                        nc.gpsimd.tensor_tensor(colh_lo[:, at], h, colh_hi[:, at].bitcast(F32),
                                                ALU.subtract).then_inc(colh_ready, 1)

                pool.wait_ge(h0_ready, 1)
                split_rows(0, 0, 0)
                with pool.Fori(0, CB) as c:
                    split_columns(c)
                    with pool.Fori(0, IB // 2) as p:
                        for par in range(2):
                            n = IB * c + 2 * p + par
                            b = (2 * p + par + 1) & (IB - 1)
                            pool.wait_ge(h0_ready, b // 2 + 1)
                            split_rows(n + 1, b, 1 - par)

        with ExitStack() as ctx:
            def sb(name, shape, dt=F32):
                return ctx.enter_context(nc.sbuf_tensor(name, shape, dt))

            def sem(name):
                return ctx.enter_context(nc.semaphore(name))

            DE = D + 1
            SUBS = NT // 2
            CH = 8
            CHUNKS = NT // CH
            CSUB = CH // 2

            x1 = sb("x1", [P, NT, D])
            hv = sb("hv", [P, NT, DE])
            win = sb("win", [P, D])
            wout = sb("wout", [P, D])
            watt = sb("watt", [P, DE])
            watt_t = sb("watt_t", [P, D])
            a1col = sb("a1col", [P, 1])
            a2col = sb("a2col", [P, 1])
            bias = sb("bias", [P, 1])
            a1wide = sb("a1wide", [P, P])
            wa1 = sb("wa1", [P, P])
            ones = sb("ones", [P, P])
            mean_w = sb("mean_w", [P, P])
            degree = sb("degree", [P, 2, NT])
            positive = sb("positive", [P, 2, NT])
            guarded = sb("guarded", [P, 2, NT])
            inverse = sb("inverse", [P, 2, NT])
            z_in = sb("z_in", [P, 2, ROWS])
            z_out = sb("z_out", [P, 2, ROWS])
            hn = sb("hn", [P, 2, ROWS])
            hn_t = sb("hn_t", [P, 2, ROWS])
            h_sum = sb("h_sum", [P, IT, DE])
            h_mean = sb("h_mean", [P, D])
            top_part = sb("top_part", [P, 1])
            top_one = sb("top_one", [1, 1])
            top = sb("top", [P, 1])
            w_bias = sb("w_bias", [P, 1])
            v_bias = sb("v_bias", [P, 1])
            top_b = sb("top_b", [P, 1])
            c_bias = sb("c_bias", [P, 1])
            minus1 = sb("minus1", [P, 1])
            w_col = sb("w_col", [P, NT])
            v_col = sb("v_col", [P, NT])
            c_row = sb("c_row", [P, 2, ROWS])
            m_tile = sb("m_tile", [P, 2, CH, ROWS], U8)
            r_tile = sb("r_tile", [P, 2, 2, ROWS])
            p_tile = sb("p_tile", [P, 4, 2, ROWS])
            empty = sb("empty", [P, IT])
            denom = sb("denom", [P, IT])
            invden = sb("invden", [P, IT])
            y = sb("y", [P, 2, IT, D])
            bank = [ctx.enter_context(nc.psum_tensor(f"bank{i}", [P, 512], F32)) for i in range(8)]

            x_loaded = [sem(f"x1_loaded{i}") for i in range(CB)]
            weights_loaded = sem("weights_loaded")
            consts = sem("consts")
            watt_turned = sem("watt_turned")
            watt_t_ready = sem("watt_t_ready")
            a1wide_ready = sem("a1wide_ready")
            wa_done = sem("wa_done")
            wa_ready = sem("wa_ready")
            deg_chain = sem("deg_chain")
            z_loaded = [sem(f"z_loaded{i}") for i in range(2)]
            projected = sem("projected")
            x1_part = sem("x1_part")
            x1_ready = sem("x1_ready")
            stats_chain = sem("stats_chain")
            factors_chain = sem("factors_chain")
            stats_ready = sem("stats1_ready")
            sqrt_done = sem("sqrt1_done")
            factors_ready = sem("factors1_ready")
            hn_ready = sem("hn_ready")
            hn_turned = sem("hn_turned")
            hn_t_ready = sem("hn_t_ready")
            h_done = sem("h_done")
            h_saved = sem("h_saved")
            sum_done = sem("sum_done")
            top_chain = sem("top_chain")
            top_turned = sem("top_turned")
            top_spread = sem("top_spread")
            mean_done = sem("mean_done")
            mean_saved = sem("mean_saved")
            w_ready = sem("w_ready")
            v_ready = sem("v_ready")
            hv_ready = sem("hv_ready")
            c_raw = sem("c_raw")
            c_ready = sem("c_ready")
            m_loaded = [sem(f"m_loaded{i}") for i in range(2)]
            r_ready = sem("r_ready")
            p_ready = sem("p_ready")
            p_used = sem("p_used")
            acc_free = sem("acc_free")
            evac_chain = sem("evac_chain")
            y_ready = sem("y_ready")
            y_stored = [sem(f"y_stored{i}") for i in range(2)]
            y_free = sem("y_free")
            R_SLOTS, P_SLOTS = 2, 4

            block = ctx.enter_context(nc.Block("layer1"))

            @block.sync
            def _(sp):
                for c in range(CB):
                    if c == 0:
                        for dst, src in ((win[:, :], w_in), (wout[:, :], w_out), (watt[:, 0:D], w_att),
                                         (a1col[:, :], a1.rearrange("(d o) -> d o", o=1)),
                                         (a2col[:, :], a2.rearrange("(d o) -> d o", o=1)),
                                         (bias[:, :], a_bias.rearrange("(a o) -> a o", o=1).broadcast_to([P, 1]))):
                            sp.dma_start(dst, src).then_inc(weights_loaded, 16)
                    sp.dma_start(x1[:, bass.ts(c, LNT), :], x_rows[c]).then_inc(x_loaded[c], 16)

                def load_z(c, par):
                    sp.dma_start(z_in[:, par, :], in_sum[:, bass.ts(c, ROWS)]).then_inc(z_loaded[par], 16)
                    sp.dma_start(z_out[:, par, :], out_sum[:, bass.ts(c, ROWS)]).then_inc(z_loaded[par], 16)

                load_z(0, 0)
                load_z(1, 1)
                with sp.Fori(1, IB // 2) as g:
                    for par in range(2):
                        wait_alone(sp, projected, 2 * g + par - 1)
                        load_z(2 * g + par, par)

                def load_mask(b, chunk, s):
                    sp.dma_start(m_tile[:, s, :, :], mask_dram[b, :, bass.ds(chunk * CH, CH), :]) \
                        .then_inc(m_loaded[s], 16)

                load_mask(0, 0, 0)
                load_mask(0, 1, 1)
                with sp.Fori(1, IB * CHUNKS // 2) as g:
                    for s in range(2):
                        n = 2 * g + s
                        wait_alone(sp, p_ready, R_SLOTS + CSUB * (n - 1))
                        load_mask(n // CHUNKS, n & (CHUNKS - 1), s)

            @block.tensor
            def _(pe):
                pe.wait_ge(weights_loaded, 96)
                pe.transpose(bank[0][:, 0:D], watt[:, 0:D], ident[:, :]).then_inc(watt_turned, 1)
                pe.wait_ge(watt_t_ready, 1)
                pe.wait_ge(a1wide_ready, 1)
                pe.matmul(bank[1][:, 0:P], watt_t[:, :], a1wide[:, :], start=True, stop=True)
                pe.matmul(bank[2][:, 0:1], watt_t[:, :], a2col[:, :], start=True, stop=True).then_inc(wa_done, 1)
                pe.wait_ge(wa_ready, 2)

                def project(c, par):
                    pe.wait_ge(z_loaded[par], 32 * (c // 2 + 1))
                    pe.wait_ge(x1_ready, c + 1)
                    for t in range(IT):
                        pe.matmul(bank[par][:, bass.ts(t, D)], z_in[:, par, bass.ts(t, P)], win[:, :],
                                  start=True, stop=True)
                        ins = pe.matmul(bank[2 + par][:, bass.ts(t, D)], z_out[:, par, bass.ts(t, P)], wout[:, :],
                                        start=True, stop=True)
                    ins.then_inc(projected, 1)

                def turn_hn(c, par):
                    pe.wait_ge(hn_ready, 2 + c + 1)
                    for t in range(IT):
                        ins = pe.transpose(bank[4][:, bass.ts(t, P)], hn[:, par, bass.ts(t, P)], ident[:, :])
                    ins.then_inc(hn_turned, 1)

                def attend_inputs(c, par):
                    pe.wait_ge(hn_t_ready, c + 1)
                    pe.wait_ge(h_saved, c + 1)
                    pe.matmul(bank[5][:, 0:ROWS], wa1[:, :], hn_t[:, par, :], start=True, stop=True)
                    for t in range(IT):
                        ins = pe.matmul(bank[6 + t // 2][:, bass.ts(t % 2, DE)], hn_t[:, par, bass.ts(t, P)],
                                        watt[:, :], start=True, stop=True)
                    ins.then_inc(h_done, 1)

                project(0, 0)
                project(1, 1)
                project(2, 0)
                turn_hn(0, 0)
                project(3, 1)
                attend_inputs(0, 0)
                turn_hn(1, 1)
                with pe.Fori(2, IB // 2) as g:
                    for par in range(2):
                        c = 2 * g + par
                        project(c, par)
                        attend_inputs(c - 3, 1 - par)
                        turn_hn(c - 2, par)
                for c in range(IB - 3, IB):
                    attend_inputs(c, c % 2)
                    if c + 1 < IB:
                        turn_hn(c + 1, (c + 1) % 2)

                pe.wait_ge(top_chain, 1)
                pe.transpose(bank[0][0:1, 0:P], top_part[:, :], ident[:, :]).then_inc(top_turned, 1)
                pe.wait_ge(top_chain, 2)
                pe.matmul(bank[1][:, 0:1], ones[0:1, :], top_one[:, :], start=True, stop=True).then_inc(top_spread, 1)
                pe.wait_ge(sum_done, IB + 1)
                for t in range(IT):
                    ins = pe.matmul(bank[2][:, 0:D], mean_w[:, :], h_sum[:, t, 0:D], start=(t == 0), stop=(t == IT - 1))
                ins.then_inc(mean_done, 1)
                pe.wait_ge(mean_saved, 1)

                def chunk(b, ch, s, par, first):
                    for i in range(CSUB):
                        j = ch * CSUB + i
                        k = (s * CSUB + i) % P_SLOTS
                        pe.wait_ge(p_ready, R_SLOTS + b * SUBS + j + 1)
                        for half in range(2):
                            for t in range(IT):
                                ins = pe.matmul(bank[IT * par + t][:, 0:DE], p_tile[:, k, half, bass.ts(t, P)],
                                                hv[:, 2 * j + half, :],
                                                start=(first and i == 0 and half == 0), stop=(i == CSUB - 1 and half == 1),
                                                skip_group_check=True)
                        ins.then_inc(p_used, 1)

                with pe.Fori(0, IB // 2) as g:
                    for par in range(2):
                        b = 2 * g + par
                        pe.wait_ge(acc_free, b + 1)
                        for s in range(2):
                            pe.wait_ge(hv_ready, s + 1)
                            chunk(b, s, s, par, s == 0)
                        with pe.Fori(1, CHUNKS // 2) as cp:
                            for s in range(2):
                                pe.wait_ge(hv_ready, 2 * cp + s + 1)
                                chunk(b, 2 * cp + s, s, par, False)

            @block.scalar
            def _(act):
                act.wait_ge(watt_turned, 1)
                nc.scalar.copy(watt_t[:, :], bank[0][:, 0:D]).then_inc(watt_t_ready, 1)
                act.wait_ge(wa_done, 1)
                nc.scalar.copy(wa1[:, :], bank[1][:, 0:P]).then_inc(wa_ready, 1)
                nc.scalar.copy(watt[:, D:DE], bank[2][:, 0:1]).then_inc(wa_ready, 1)

                def root(c, par):
                    act.wait_ge(stats_ready, c + 1)
                    nc.scalar.activation(std[:, par, 0:IT], moments[:, par, 0:IT, 1], ACT.Sqrt, bias=eps[:, 0:1]) \
                        .then_inc(sqrt_done, 1)

                def normalise(c, par):
                    act.wait_ge(factors_ready, c + 1)
                    for t in range(IT):
                        ins = nc.scalar.activation(hn[:, par, bass.ts(t, P)], x1[:, c * IT + t, :], ACT.Relu,
                                                   bias=shift[:, par, t:t + 1], scale=rstd[:, par, t:t + 1])
                    ins.then_inc(hn_ready, 1)

                def copy_turned(c, par):
                    act.wait_ge(hn_turned, c + 1)
                    nc.scalar.copy(hn_t[:, par, :], bank[4][:, :]).then_inc(hn_t_ready, 1)

                def save(c):
                    act.wait_ge(h_done, c + 1)
                    nc.scalar.copy(in_sum[:, bass.ts(c, ROWS)], bank[5][:, :])
                    for half in range(2):
                        ins = nc.scalar.copy(hv[:, bass.ds(c * IT + 2 * half, 2), :],
                                             bank[6 + half][:, 0:2 * DE].rearrange("p (t d) -> p t d", d=DE))
                    ins.then_inc(h_saved, 1)

                root(0, 0)
                root(1, 1)
                normalise(0, 0)
                root(2, 0)
                normalise(1, 1)
                copy_turned(0, 0)
                root(3, 1)
                normalise(2, 0)
                save(0)
                with act.Fori(2, IB // 2) as g:
                    for par in range(2):
                        c = 2 * g + par
                        copy_turned(c - 3, 1 - par)
                        root(c, par)
                        normalise(c - 1, 1 - par)
                        save(c - 3)
                for c in range(IB - 3, IB):
                    copy_turned(c, c % 2)
                    if c == IB - 3:
                        normalise(IB - 1, 1)
                    save(c)

                s2 = hv[:, :, D]
                act.wait_ge(top_chain, 6)
                nc.scalar.activation(w_col[:, :], s2, ACT.Exp, bias=w_bias[:, 0:1], scale=1 - SLOPE).then_inc(w_ready, 1)
                nc.scalar.activation(v_col[:, :], s2, ACT.Exp, bias=v_bias[:, 0:1], scale=SLOPE).then_inc(v_ready, 1)

                def c_of(b, par):
                    nc.scalar.activation(c_row[:, par, :], in_sum[:, bass.ts(b, ROWS)], ACT.Exp,
                                         bias=c_bias[:, 0:1], scale=1 - SLOPE).then_inc(c_raw, 1)

                def chunk(b, ch, s, par):
                    for i in range(CSUB):
                        j = ch * CSUB + i
                        act.wait_ge(p_ready, b * SUBS + j + 1)
                        for half in range(2):
                            ins = nc.scalar.activation(r_tile[:, i % 2, half, :], c_row[:, par, :], ACT.Relu,
                                                       bias=minus1[:, 0:1], scale=w_col[:, bass.ds(2 * j + half, 1)])
                        ins.then_inc(r_ready, 1)

                c_of(0, 0)
                act.wait_ge(w_ready, 1)
                with act.Fori(0, IB // 2) as g:
                    for par in range(2):
                        b = 2 * g + par
                        act.wait_ge(c_ready, b + 1)
                        chunk(b, 0, 0, par)
                        c_of((b + 1) & (IB - 1), 1 - par)
                        with act.Fori(1, CHUNKS) as ch:
                            chunk(b, ch, 0, par)

            @block.vector
            def _(dve):
                dve.memset(minus1[:, :], -1.0)
                dve.memset(ones[:, :], 1.0)
                dve.memset(mean_w[:, :], 1.0 / N).then_inc(consts, 1)
                dve.sem_inc(x1_ready, 2)
                dve.sem_inc(hn_ready, 2)
                dve.sem_inc(h_saved, 1)
                dve.sem_inc(y_free, 2)
                dve.sem_inc(p_ready, R_SLOTS)
                dve.sem_inc(acc_free, 2)
                dve.wait_ge(consts, 1)
                dve.wait_ge(weights_loaded, 96)
                dve.tensor_scalar(a1wide[:, :], ones[:, :], a1col[:, 0:1], None, ALU.mult).then_inc(a1wide_ready, 1)

                dve.tensor_reduce(degree[:, 0, :], row_parts[:, :, :], AX_X, ALU.add)
                dve.tensor_reduce(degree[:, 1, :], col_parts[:, :, :], AX_X, ALU.add).then_inc(deg_chain, 1)
                dve.wait_ge(deg_chain, 1)
                dve.tensor_scalar(positive[:, :, :], degree[:, :, :], 0.0, None, ALU.is_gt).then_inc(deg_chain, 1)
                dve.wait_ge(deg_chain, 2)
                dve.tensor_tensor(guarded[:, :, :], degree[:, :, :], positive[:, :, :], ALU.mult).then_inc(deg_chain, 1)
                dve.wait_ge(deg_chain, 3)
                dve.scalar_tensor_tensor(out=guarded[:, :, :].rearrange("p a b -> p (a b)"),
                                         in0=guarded[:, :, :].rearrange("p a b -> p (a b)"), scalar=1.0,
                                         in1=positive[:, :, :].rearrange("p a b -> p (a b)"),
                                         op0=ALU.add, op1=ALU.subtract).then_inc(deg_chain, 1)
                dve.wait_ge(deg_chain, 4)
                dve.reciprocal(inverse[:, :, :], guarded[:, :, :]).then_inc(deg_chain, 1)
                dve.wait_ge(deg_chain, 5)

                def residual(c, par):
                    dve.wait_ge(projected, c + 1)
                    for t in range(IT):
                        row = x1[:, c * IT + t, :]
                        ins = dve.scalar_tensor_tensor(out=row, in0=bank[par][:, bass.ts(t, D)],
                                                       scalar=inverse[:, 0, bass.ds(c * IT + t, 1)], in1=row,
                                                       op0=ALU.mult, op1=ALU.add)
                    ins.then_inc(x1_part, 1)
                    dve.wait_ge(x1_part, c + 1)
                    for t in range(IT):
                        row = x1[:, c * IT + t, :]
                        ins = dve.scalar_tensor_tensor(out=row, in0=bank[2 + par][:, bass.ts(t, D)],
                                                       scalar=inverse[:, 1, bass.ds(c * IT + t, 1)], in1=row,
                                                       op0=ALU.mult, op1=ALU.add)
                    ins.then_inc(x1_ready, 1)
                    wait_alone(dve, x1_ready, 2 + c + 1)
                    norm_stats(dve, IT, par, lambda t: x1[:, c * IT + t, :], stats_chain, c, stats_ready)

                def factors(c, par):
                    dve.wait_ge(hn_ready, c + 1)
                    dve.wait_ge(sqrt_done, c + 1)
                    norm_factors(dve, IT, par, factors_chain, FACTORS_CHAIN * c, factors_ready)

                for c in range(CB):
                    dve.wait_ge(x_loaded[c], 16)
                residual(0, 0)
                residual(1, 1)
                factors(0, 0)
                with dve.Fori(1, IB // 2) as g:
                    for par in range(2):
                        c = 2 * g + par
                        residual(c, par)
                        factors(c - 1, 1 - par)
                factors(IB - 1, 1)

                dve.wait_ge(h_saved, 1 + IB)
                dve.tensor_reduce(top_part[:, :], hv[:, :, D], AX_X, ALU.max).then_inc(top_chain, 1)
                dve.wait_ge(top_turned, 1)
                dve.tensor_reduce(top_one[:, :], bank[0][0:1, 0:P], AX_X, ALU.max).then_inc(top_chain, 1)
                dve.wait_ge(top_spread, 1)
                dve.tensor_copy(top[:, :], bank[1][:, 0:1]).then_inc(top_chain, 1)
                dve.wait_ge(top_chain, 3)
                dve.tensor_scalar(w_bias[:, :], top[:, :], SLOPE - 1, None, ALU.mult)
                dve.tensor_scalar(v_bias[:, :], top[:, :], -SLOPE, None, ALU.mult).then_inc(top_chain, 1)
                dve.tensor_tensor(top_b[:, :], top[:, :], bias[:, :], ALU.add).then_inc(top_chain, 1)
                dve.wait_ge(top_chain, 5)
                dve.tensor_scalar(c_bias[:, :], top_b[:, :], 1 - SLOPE, None, ALU.mult).then_inc(top_chain, 1)
                dve.wait_ge(mean_done, 1)
                dve.tensor_copy(h_mean[:, :], bank[2][:, 0:D]).then_inc(mean_saved, 1)

                def cap(b, par):
                    dve.wait_ge(c_raw, b + 1)
                    dve.tensor_scalar(c_row[:, par, :], c_row[:, par, :], CAP, None, ALU.min).then_inc(c_ready, 1)

                def chunk(b, ch, s):
                    for i in range(CSUB):
                        q = b * SUBS + ch * CSUB + i
                        k = (s * CSUB + i) % P_SLOTS
                        dve.wait_ge(r_ready, q + 1)
                        dve.wait_ge(p_used, q + 1)
                        dve.scalar_tensor_tensor(out=p_tile[:, k, :, :].rearrange("p a b -> p (a b)"),
                                                 in0=r_tile[:, i % 2, :, :].rearrange("p a b -> p (a b)"), scalar=1.0,
                                                 in1=m_tile[:, s, 2 * i:2 * i + 2, :].rearrange("p a b -> p (a b)"),
                                                 op0=ALU.add, op1=ALU.mult).then_inc(p_ready, 1)

                EVAC = 3

                def finish(b, par):
                    dve.wait_ge(p_used, P_SLOTS + SUBS * (b + 1))
                    for t in range(IT):
                        ins = dve.tensor_scalar(empty[:, t:t + 1], bank[IT * par + t][:, D:DE], 0.0, None, ALU.is_equal)
                    ins.then_inc(evac_chain, 1)
                    dve.wait_ge(evac_chain, EVAC * b + 1)
                    for t in range(IT):
                        ins = dve.tensor_tensor(denom[:, t:t + 1], bank[IT * par + t][:, D:DE], empty[:, t:t + 1], ALU.add)
                    ins.then_inc(evac_chain, 1)
                    dve.wait_ge(evac_chain, EVAC * b + 2)
                    dve.reciprocal(invden[:, :], denom[:, :]).then_inc(evac_chain, 1)
                    dve.wait_ge(evac_chain, EVAC * b + 3)
                    dve.wait_ge(y_free, b + 1)
                    for t in range(IT):
                        ins = dve.scalar_tensor_tensor(out=y[:, par, t, :], in0=bank[IT * par + t][:, 0:D],
                                                       scalar=invden[:, t:t + 1], in1=x1[:, b * IT + t, :],
                                                       op0=ALU.mult, op1=ALU.add)
                    ins.then_inc(acc_free, 1)
                    dve.wait_ge(acc_free, 2 + b + 1)
                    for t in range(IT):
                        ins = dve.scalar_tensor_tensor(out=y[:, par, t, :], in0=h_mean[:, :], scalar=empty[:, t:t + 1],
                                                       in1=y[:, par, t, :], op0=ALU.mult, op1=ALU.add)
                    ins.then_inc(y_ready, 1)

                def row_block(g, par, first):
                    b = 2 * g + par
                    for s in range(2):
                        dve.wait_ge(m_loaded[s], 16 * (b * CHUNKS // 2 + 1))
                        chunk(b, s, s)
                    cap(b + 1, 1 - par)
                    if not first:
                        finish(b - 1, 1 - par)
                    with dve.Fori(1, CHUNKS // 2) as cp:
                        for s in range(2):
                            dve.wait_ge(m_loaded[s], 16 * (b * CHUNKS // 2 + cp + 1))
                            chunk(b, 2 * cp + s, s)

                dve.wait_ge(mean_saved, 1)
                cap(0, 0)
                row_block(0, 0, True)
                row_block(0, 1, False)
                with dve.Fori(1, IB // 2) as g:
                    for par in range(2):
                        row_block(g, par, False)
                finish(IB - 1, 1)

            @block.gpsimd
            def _(pool):
                pool.sem_inc(p_used, P_SLOTS)
                nc.gpsimd.memset(h_sum[:, :, :], 0.0).then_inc(sum_done, 1)

                def add_h(c):
                    pool.wait_ge(h_saved, 1 + c + 1)
                    wait_alone(pool, sum_done, c + 1)
                    nc.gpsimd.tensor_tensor(h_sum[:, :, :], h_sum[:, :, :], hv[:, bass.ds(c * IT, IT), :],
                                            ALU.add).then_inc(sum_done, 1)

                with pool.Fori(0, IB) as c:
                    add_h(c)

                pool.wait_ge(sum_done, IB + 1)
                pool.wait_ge(v_ready, 1)
                for ch in range(CHUNKS):
                    at = slice(ch * CH, ch * CH + CH)
                    v = v_col[:, at].rearrange("p (t o) -> p t o", o=1)
                    nc.gpsimd.tensor_tensor(hv[:, at, 0:D], hv[:, at, 0:D], v.broadcast_to([P, CH, D]), ALU.mult)
                    nc.gpsimd.tensor_copy(hv[:, at, D:DE], v).then_inc(hv_ready, 1)

                def store(g, par):
                    b = 2 * g + par
                    pool.wait_ge(y_ready, b + 1)
                    pool.dma_start(out_rows[b], y[:, par, :, :]).then_inc(y_stored[par], 16)
                    pool.wait_ge(y_stored[par], 16 * (g + 1))
                    pool.sem_inc(y_free, 1)

                with pool.Fori(0, IB // 2) as g:
                    for par in range(2):
                        store(g, par)


_INS = ["x", "adj", "L0_gnn_W_in", "L0_gnn_W_out", "L1_gnn_W", "L1_gnn_a1", "L1_gnn_a2", "L1_gnn_a_bias"]


def kernel(**inputs):
    import numpy as _np
    import concourse.bacc as _bacc
    from concourse import mybir as _mybir
    from concourse.bass_utils import run_bass_kernel_spmd as _run

    nc = _bacc.Bacc("TRN2", target_bir_lowering=False, num_devices=1)
    arrays, args = {}, []
    for name in _INS:
        a = _np.ascontiguousarray(inputs[name])
        arrays[f"in_{name}_dram"] = a
        args.append(nc.dram_tensor(f"in_{name}_dram", a.shape, _mybir.dt.from_np(a.dtype), kind="ExternalInput").ap())
    out = nc.dram_tensor("out_0_dram", inputs["x"].shape, _mybir.dt.float32, kind="ExternalOutput").ap()
    graph_layers(nc, *args, out)
    r = _run(nc, [arrays], core_ids=[0])
    return r.results[0]["out_0_dram"]
```

```python
from contextlib import ExitStack

import concourse.bass as bass
from concourse import mybir

F32 = mybir.dt.float32
F32R = mybir.dt.float32r
U8 = mybir.dt.uint8
ALU = mybir.AluOpType
ACT = mybir.ActivationFunctionType
AX_X = mybir.AxisListType.X

P = 128
EPS = 1e-5
SLOPE = 0.2
CAP = float(2.0 ** 90)


def graph_layers(nc, x, adj, w_in, w_out, w_att, a1, a2, a_bias, out):
    N, D = x.shape
    assert D == P
    NT = N // P
    IT = 4
    ROWS = IT * P
    IB = N // ROWS
    JT = 8
    COLS = JT * P
    CB = N // COLS
    STEPS = CB * IB
    SUB = JT // 2
    LNT = 8
    assert SUB == IT and CB * LNT == NT and IB == 2 * CB

    x_rows = x.rearrange("(c t p) d -> c p t d", p=P, t=LNT)
    adj_v = adj.rearrange("(b t p) (c w) -> b c p t w", t=IT, p=P, w=COLS)
    mask_dram = nc.dram_tensor("mask_scratch", (IB, P, NT, ROWS), U8, kind="Internal").ap()
    out_rows = out.rearrange("(b t p) d -> b p t d", t=IT, p=P)

    with ExitStack() as whole:
        def keep(name, shape, dt=F32):
            return whole.enter_context(nc.sbuf_tensor(name, shape, dt))

        in_sum = keep("in_sum", [P, N])
        out_sum = keep("out_sum", [P, N])
        row_parts = keep("row_parts", [P, NT, CB])
        col_parts = keep("col_parts", [P, NT, IB])
        ident = keep("ident", [P, P])
        table_probe = keep("table_probe", [P, 1])
        eps = keep("eps", [P, 1])
        stats = keep("stats", [P, LNT, 6])
        moments = keep("moments", [P, LNT, 2])
        std = keep("std", [P, LNT])
        rstd0 = keep("rstd0", [P, LNT])
        newton = keep("newton", [P, LNT])
        rstd = keep("rstd", [P, LNT])
        shift = keep("shift", [P, LNT])
        win = keep("win", [P, D])
        wout = keep("wout", [P, D])
        watt = keep("watt", [P, D + 1])
        a1col = keep("a1col", [P, 1])
        a2col = keep("a2col", [P, 1])
        bias = keep("bias", [P, 1])

        weights_loaded = whole.enter_context(nc.semaphore("weights_loaded"))
        waits_done = whole.enter_context(nc.semaphore("waits_done"))

        def wait_alone(eng, sem, value):
            eng.wait_ge(sem, value)
            eng.sem_inc(waits_done, 1)

        STATS_CHAIN, FACTORS_CHAIN = 1, 5

        def norm_stats(dve, row_tile, chain, before, stats_ready):
            for t in range(LNT):
                ins = dve.bn_stats(stats[:, t, :], row_tile(t))
            ins.then_inc(chain, 1)
            wait_alone(dve, chain, before + 1)
            for t in range(LNT):
                ins = dve.bn_aggr(moments[:, t, :], stats[:, t, :])
            ins.then_inc(stats_ready, 1)

        def norm_root(act, c, stats_ready, sqrt_done):
            act.wait_ge(stats_ready, c + 1)
            nc.scalar.activation(std[:, :], moments[:, :, 1], ACT.Sqrt, bias=eps[:, 0:1]).then_inc(sqrt_done, 1)

        def norm_factors(dve, chain, before, factors_ready):
            dve.reciprocal(rstd0[:, :], std[:, :]).then_inc(chain, 1)
            dve.wait_ge(chain, before + 1)
            dve.tensor_tensor(newton[:, :], rstd0[:, :], rstd0[:, :], ALU.mult).then_inc(chain, 1)
            dve.wait_ge(chain, before + 2)
            dve.scalar_tensor_tensor(out=newton[:, :], in0=moments[:, :, 1], scalar=EPS,
                                     in1=newton[:, :], op0=ALU.add, op1=ALU.mult).then_inc(chain, 1)
            dve.wait_ge(chain, before + 3)
            dve.tensor_scalar(newton[:, :], newton[:, :], -0.5, 1.5, ALU.mult, ALU.add).then_inc(chain, 1)
            dve.wait_ge(chain, before + 4)
            dve.tensor_tensor(rstd[:, :], rstd0[:, :], newton[:, :], ALU.mult).then_inc(chain, 1)
            dve.wait_ge(chain, before + 5)
            dve.scalar_tensor_tensor(out=shift[:, :], in0=moments[:, :, 0], scalar=-1.0,
                                     in1=rstd[:, :], op0=ALU.mult, op1=ALU.mult).then_inc(factors_ready, 1)

        with ExitStack() as ctx:
            def sb(name, shape, dt=F32):
                return ctx.enter_context(nc.sbuf_tensor(name, shape, dt))

            def sem(name):
                return ctx.enter_context(nc.semaphore(name))

            h0 = sb("h0", [P, N])
            a_tile = sb("a_tile", [P, 2, IT, COLS])
            lie_hi = sb("lie_hi", [P, 2, COLS], F32R)
            lie_lo = sb("lie_lo", [P, 2, COLS], F32R)
            turn_hi = sb("turn_hi", [P, 2, 2, ROWS], F32R)
            turn_lo = sb("turn_lo", [P, 2, 2, ROWS], F32R)
            mask = sb("mask", [P, 2, JT, ROWS], U8)
            rowh_hi = sb("rowh_hi", [P, 2, ROWS], F32R)
            rowh_lo = sb("rowh_lo", [P, 2, ROWS], F32R)
            colh_hi = sb("colh_hi", [P, COLS], F32R)
            colh_lo = sb("colh_lo", [P, COLS], F32R)
            turned = ctx.enter_context(nc.psum_tensor("turned", [P, 2, 2, ROWS], F32))
            acc_in = ctx.enter_context(nc.psum_tensor("acc_in", [P, 2, ROWS], F32))
            acc_out = ctx.enter_context(nc.psum_tensor("acc_out", [P, 2, COLS // 2], F32))

            TURN_SLOTS = LIE_SLOTS = ACC_SLOTS = 2
            LIE_CREDIT = 2 * SUB
            MASK_CREDIT = 16
            NORM_STATS, NORM_ROOT, NORM_FACTORS = (0, 1), (0, 3), (0, 4)
            NORM_TILES = {(0, 5): (0, 1), (0, 6): (2, 3), (0, 7): (4, 5), (1, 0): (6, 7)}
            ORDER = [(True, 0), (True, 1), (False, 0), (False, 1), (True, 2), (False, 2), (True, 3), (False, 3)]
            x_loaded = [sem(f"x_loaded{c}") for c in range(CB)]
            a_loaded = [sem(f"a_loaded{i}") for i in range(2)]
            mask_stored = [sem(f"mask_stored{i}") for i in range(2)]
            ident_zero = sem("ident_zero")
            ident_ready = sem("ident_ready")
            eps_ready = sem("eps_ready")
            sum_cleared = sem("sum_cleared")
            ln_chain = sem("ln_chain")
            stats_ready = sem("stats_ready")
            sqrt_done = sem("sqrt_done")
            factors_ready = sem("factors_ready")
            h0_ready = sem("h0_ready")
            rowh_hi_done = sem("rowh_hi_done")
            rowh_ready = sem("rowh_ready")
            colh_hi_done = sem("colh_hi_done")
            colh_ready = sem("colh_ready")
            turned_done = sem("turned_done")
            turn_hi_done = sem("turn_hi_done")
            turn_ready = sem("turn_ready")
            turn_used = sem("turn_used")
            mask_done = sem("mask_done")
            lie_hi_done = sem("lie_hi_done")
            lie_ready = sem("lie_ready")
            lie_used = sem("lie_used")
            in_added = sem("in_added")
            out_saved = sem("out_saved")

            weights = ((watt[:, 0:D], w_att),
                       (a1col[:, :], a1.rearrange("(d o) -> d o", o=1)),
                       (a2col[:, :], a2.rearrange("(d o) -> d o", o=1)),
                       (win[:, :], w_in), (wout[:, :], w_out),
                       (bias[:, :], a_bias.rearrange("(a o) -> a o", o=1).broadcast_to([P, 1])))

            block = ctx.enter_context(nc.Block("layer0"))

            @block.sync
            def _(sp):
                def load(b, c, par):
                    sp.dma_start(a_tile[:, par, :, :], adj_v[b, c]).then_inc(a_loaded[par], 16)

                def store_mask(n, b, c, par):
                    wait_alone(sp, mask_done, TURN_SLOTS + SUB * (n + 1))
                    sp.dma_start(mask_dram[b, :, bass.ds(c * JT, JT), :], mask[:, par, :, :]) \
                        .then_inc(mask_stored[par], 16)

                def load_x(c):
                    sp.dma_start(out_sum[:, bass.ts(c, LNT * P)].rearrange("p (t d) -> p t d", d=P), x_rows[c]) \
                        .then_inc(x_loaded[c], 16)

                load_x(0)
                load(0, 0, 0)
                load_x(1)
                load(1, 0, 1)
                for c in range(2, CB):
                    load_x(c)
                for dst, src in weights:
                    sp.dma_start(dst, src).then_inc(weights_loaded, 16)
                with sp.Fori(1, STEPS // 2) as g:
                    for par in range(2):
                        n = 2 * g + par
                        sp.wait_ge(turned_done, SUB * (n - 1))
                        wait_alone(sp, lie_ready, SUB * (n - 1))
                        load(n & (IB - 1), n // IB, par)
                        store_mask(n - 2, (n - 2) & (IB - 1), (n - 2) // IB, par)
                for par in range(2):
                    store_mask(STEPS - 2 + par, IB - 2 + par, CB - 1, par)
                for par in range(2):
                    sp.wait_ge(mask_stored[par], MASK_CREDIT + 16 * (STEPS // 2))

            @block.tensor
            def _(pe):
                def turn(n, u, par):
                    m = SUB * n + u
                    pe.wait_ge(turn_ready, m + 1)
                    for k in range(2):
                        for t in range(IT):
                            ins = pe.transpose(turned[:, u % 2, k, bass.ts(t, P)],
                                               a_tile[:, par, t, bass.ts(2 * u + k, P)], ident[:, :])
                    ins.then_inc(turned_done, 1)

                def lying_product(n, u, par, first):
                    pe.wait_ge(lie_ready, SUB * n + u + 1)
                    hi, lo = (h[:, par, bass.ts(u, P)] for h in (rowh_hi, rowh_lo))
                    s = u % 2
                    for i, (h, a) in enumerate(((hi, lie_hi), (hi, lie_lo), (lo, lie_hi))):
                        for half in range(2):
                            ins = pe.matmul(acc_out[:, half, :], h, a[:, s, bass.ts(half, COLS // 2)],
                                            start=(first and u == 0 and i == 0), stop=(i == 2),
                                            skip_group_check=True)
                    ins.then_inc(lie_used, 1)

                def turned_product(n, u, par, c):
                    pe.wait_ge(turn_ready, TURN_SLOTS + SUB * n + u + 1)
                    pe.wait_ge(colh_ready, SUB * c + u + 1)
                    s = u % 2
                    for k in range(2):
                        hi, lo = (h[:, bass.ts(2 * u + k, P)] for h in (colh_hi, colh_lo))
                        for i, (h, a) in enumerate(((hi, turn_hi), (hi, turn_lo), (lo, turn_hi))):
                            ins = pe.matmul(acc_in[:, par, :], h, a[:, s, k, :],
                                            start=(u == 0 and k == 0 and i == 0),
                                            stop=(u == SUB - 1 and k == 1 and i == 2))
                    ins.then_inc(turn_used, 1)

                def pair(c, p, first):
                    for par in range(2):
                        n = IB * c + 2 * p + par
                        new = first and par == 0
                        pe.wait_ge(a_loaded[par], 16 * ((IB // 2) * c + p + 1))
                        turn(n, 0, par)
                        pe.wait_ge(rowh_ready, n + 1)
                        if new:
                            pe.wait_ge(out_saved, c + 1)
                        lying_product(n, 0, par, new)
                        turn(n, 1, par)
                        lying_product(n, 1, par, False)
                        pe.wait_ge(in_added, n + 1)
                        turned_product(n, 0, par, c)
                        turn(n, 2, par)
                        turned_product(n, 1, par, c)
                        turn(n, 3, par)
                        for u in range(2, SUB):
                            lying_product(n, u, par, False)
                            turned_product(n, u, par, c)

                pe.wait_ge(ident_ready, 1)
                with pe.Fori(0, CB) as c:
                    pair(c, 0, True)
                    with pe.Fori(1, IB // 2) as p:
                        pair(c, p, False)

            @block.scalar
            def _(act):
                act.wait_ge(eps_ready, 1)
                nc.scalar.activation(table_probe[:, :], eps[:, :], ACT.Sqrt)

                def normalise(c, tiles):
                    act.wait_ge(factors_ready, c + 1)
                    for t in tiles:
                        at = bass.ds((c * LNT + t) * P, P)
                        ins = nc.scalar.activation(h0[:, at], out_sum[:, at], ACT.Relu,
                                                   bias=shift[:, t:t + 1], scale=rstd[:, t:t + 1])
                        if t % IT == IT - 1:
                            ins.then_inc(h0_ready, 1)

                def pair(c, p, norm=None):
                    for par in range(2):
                        n = IB * c + 2 * p + par
                        b = 2 * p + par
                        act.wait_ge(a_loaded[par], 16 * ((IB // 2) * c + p + 1))
                        for item, (lying, u) in enumerate(ORDER):
                            if norm is not None and (par, item) == NORM_ROOT:
                                norm_root(act, norm, stats_ready, sqrt_done)
                            if norm is not None and (par, item) in NORM_TILES:
                                normalise(norm, NORM_TILES[par, item])
                            m = SUB * n + u
                            s = u % 2
                            if lying:
                                act.wait_ge(lie_used, m + LIE_CREDIT - LIE_SLOTS + 1)
                                nc.scalar.activation(lie_hi[:, s, :], a_tile[:, par, u, :], ACT.Copy,
                                                     accum_out=row_parts[:, b * IT + u, bass.ds(c, 1)]) \
                                    .then_inc(lie_hi_done, 1)
                                continue
                            act.wait_ge(turned_done, m + 1)
                            act.wait_ge(turn_used, m + 1)
                            act.wait_ge(mask_done, m + 1)
                            for k in range(2):
                                ins = nc.scalar.activation(
                                    turn_hi[:, s, k, :], turned[:, s, k, :], ACT.Copy,
                                    accum_out=col_parts[:, c * JT + 2 * u + k, bass.ds(b, 1)])
                            ins.then_inc(turn_hi_done, 1)

                def save_out(c):
                    act.wait_ge(lie_used, LIE_CREDIT + SUB * IB * (c + 1))
                    nc.scalar.copy(out_sum[:, bass.ts(c, COLS)], acc_out[:, :, :].rearrange("p a b -> p (a b)")) \
                        .then_inc(out_saved, 1)

                norm_root(act, 0, stats_ready, sqrt_done)
                normalise(0, range(LNT))
                with act.Fori(0, CB - 1) as p:
                    pair(0, p, p + 1)
                pair(0, CB - 1)
                save_out(0)
                with act.Fori(1, CB) as c:
                    with act.Fori(0, IB // 2) as p:
                        pair(c, p)
                    save_out(c)

            @block.vector
            def _(dve):
                dve.memset(eps[:, :], EPS).then_inc(eps_ready, 1)
                dve.sem_inc(turn_ready, TURN_SLOTS)
                dve.sem_inc(in_added, ACC_SLOTS)

                def layer_stats(c):
                    norm_stats(dve, lambda t: out_sum[:, bass.ds((c * LNT + t) * P, P)],
                               ln_chain, (STATS_CHAIN + FACTORS_CHAIN) * c, stats_ready)

                def layer_factors(c):
                    dve.wait_ge(sqrt_done, c + 1)
                    norm_factors(dve, ln_chain, (STATS_CHAIN + FACTORS_CHAIN) * c + STATS_CHAIN,
                                 factors_ready)

                def add_in(n, b, par):
                    dve.wait_ge(turn_used, TURN_SLOTS + SUB * (n + 1))
                    rows = in_sum[:, bass.ts(b, ROWS)]
                    dve.tensor_tensor(rows, acc_in[:, par, :], rows, ALU.add).then_inc(in_added, 1)

                def pair(c, p, norm=None, first=False):
                    for par in range(2):
                        n = IB * c + 2 * p + par
                        for item, (lying, u) in enumerate(ORDER):
                            if norm is not None and (par, item) == NORM_STATS:
                                layer_stats(norm)
                            if norm is not None and (par, item) == NORM_FACTORS:
                                dve.wait_ge(h0_ready, 2 * norm)
                                layer_factors(norm)
                            m = SUB * n + u
                            s = u % 2
                            if lying:
                                dve.wait_ge(lie_hi_done, m + 1)
                                dve.tensor_tensor(lie_lo[:, s, :], a_tile[:, par, u, :],
                                                  lie_hi[:, s, :].bitcast(F32), ALU.subtract).then_inc(lie_ready, 1)
                                continue
                            dve.wait_ge(turn_hi_done, m + 1)
                            dve.tensor_tensor(turn_lo[:, s, :, :].rearrange("p a b -> p (a b)"),
                                              turned[:, s, :, :].rearrange("p a b -> p (a b)"),
                                              turn_hi[:, s, :, :].rearrange("p a b -> p (a b)").bitcast(F32),
                                              ALU.subtract).then_inc(turn_ready, 1)
                            if u == 0:
                                dve.wait_ge(mask_stored[par], MASK_CREDIT + 16 * ((IB // 2) * c + p))
                            dve.tensor_scalar(mask[:, par, 2 * u:2 * u + 2, :].rearrange("p a b -> p (a b)"),
                                              turn_hi[:, s, :, :].rearrange("p a b -> p (a b)").bitcast(F32),
                                              0.0, None, ALU.is_gt).then_inc(mask_done, 1)
                            if u == 1 and not (first and par == 0):
                                add_in(n - 1, (2 * p + par + IB - 1) & (IB - 1), 1 - par)

                dve.wait_ge(x_loaded[0], 16)
                layer_stats(0)
                layer_factors(0)
                dve.wait_ge(sum_cleared, 1)
                dve.wait_ge(x_loaded[1], 16)
                pair(0, 0, norm=1, first=True)
                for c in range(2, CB):
                    dve.wait_ge(x_loaded[c], 16)
                with dve.Fori(1, CB - 1) as p:
                    pair(0, p, norm=p + 1)
                pair(0, CB - 1)
                with dve.Fori(1, CB) as c:
                    with dve.Fori(0, IB // 2) as p:
                        pair(c, p)
                add_in(STEPS - 1, IB - 1, 1)

            @block.gpsimd
            def _(pool):
                pool.sem_inc(turn_used, TURN_SLOTS)
                pool.sem_inc(lie_used, LIE_CREDIT)
                pool.sem_inc(mask_done, TURN_SLOTS)
                pool.sem_inc(out_saved, 1)
                for par in range(2):
                    pool.sem_inc(mask_stored[par], MASK_CREDIT)
                nc.gpsimd.memset(ident[:, :], 0.0).then_inc(ident_zero, 1)
                pool.wait_ge(ident_zero, 1)
                nc.gpsimd.affine_select(out=ident[:, :], in_=ident[:, :], compare_op=ALU.not_equal, fill=1.0,
                                        base=0, pattern=[[-1, P]], channel_multiplier=1).then_inc(ident_ready, 1)
                nc.gpsimd.memset(in_sum[:, :], 0.0).then_inc(sum_cleared, 1)

                def split_rows(n, b, par):
                    pool.wait_ge(lie_used, LIE_CREDIT + SUB * (n - 1))
                    h = h0[:, bass.ts(b, ROWS)]
                    nc.gpsimd.tensor_copy(rowh_hi[:, par, :], h).then_inc(rowh_hi_done, 1)
                    wait_alone(pool, rowh_hi_done, n + 1)
                    nc.gpsimd.tensor_tensor(rowh_lo[:, par, :], h, rowh_hi[:, par, :].bitcast(F32),
                                            ALU.subtract).then_inc(rowh_ready, 1)

                def split_columns(c):
                    pool.wait_ge(turn_used, TURN_SLOTS + SUB * IB * c)
                    for u in range(SUB):
                        pool.wait_ge(h0_ready, 2 * c + u // 2 + 1)
                        at = bass.ts(u, COLS // SUB)
                        h = h0[:, bass.ds(c * COLS + u * (COLS // SUB), COLS // SUB)]
                        nc.gpsimd.tensor_copy(colh_hi[:, at], h).then_inc(colh_hi_done, 1)
                        wait_alone(pool, colh_hi_done, SUB * c + u + 1)
                        nc.gpsimd.tensor_tensor(colh_lo[:, at], h, colh_hi[:, at].bitcast(F32),
                                                ALU.subtract).then_inc(colh_ready, 1)

                pool.wait_ge(h0_ready, 1)
                split_rows(0, 0, 0)
                with pool.Fori(0, CB) as c:
                    split_columns(c)
                    with pool.Fori(0, IB // 2) as p:
                        for par in range(2):
                            n = IB * c + 2 * p + par
                            b = (2 * p + par + 1) & (IB - 1)
                            pool.wait_ge(h0_ready, b + 1)
                            split_rows(n + 1, b, 1 - par)

        with ExitStack() as ctx:
            def sb(name, shape, dt=F32):
                return ctx.enter_context(nc.sbuf_tensor(name, shape, dt))

            def sem(name):
                return ctx.enter_context(nc.semaphore(name))

            DE = D + 1
            SUBS = NT // 2
            CH = 8
            CHUNKS = NT // CH
            CSUB = CH // 2

            x1 = sb("x1", [P, NT, D])
            hv = sb("hv", [P, NT, DE])
            watt_t = sb("watt_t", [P, D])
            a1wide = sb("a1wide", [P, P])
            wa1 = sb("wa1", [P, P])
            ones = sb("ones", [P, P])
            mean_w = sb("mean_w", [P, P])
            degree = sb("degree", [P, 2, NT])
            positive = sb("positive", [P, 2, NT])
            guarded = sb("guarded", [P, 2, NT])
            inverse = sb("inverse", [P, 2, NT])
            z_in = sb("z_in", [P, 2, ROWS])
            z_out = sb("z_out", [P, 2, ROWS])
            hn = sb("hn", [P, 2, ROWS])
            hn_t = sb("hn_t", [P, 2, ROWS])
            h_sum = sb("h_sum", [P, IT, DE])
            h_mean = sb("h_mean", [P, D])
            top_part = sb("top_part", [P, 1])
            top_one = sb("top_one", [1, 1])
            top = sb("top", [P, 1])
            w_bias = sb("w_bias", [P, 1])
            v_bias = sb("v_bias", [P, 1])
            top_b = sb("top_b", [P, 1])
            c_bias = sb("c_bias", [P, 1])
            minus1 = sb("minus1", [P, 1])
            w_col = sb("w_col", [P, NT])
            v_col = sb("v_col", [P, NT])
            c_row = sb("c_row", [P, 2, ROWS])
            m_tile = sb("m_tile", [P, 2, CH, ROWS], U8)
            r_tile = sb("r_tile", [P, 2, 2, ROWS])
            p_tile = sb("p_tile", [P, 4, 2, ROWS])
            empty = sb("empty", [P, IT])
            denom = sb("denom", [P, IT])
            invden = sb("invden", [P, IT])
            y = sb("y", [P, 2, IT, D])
            bank = [ctx.enter_context(nc.psum_tensor(f"bank{i}", [P, 512], F32)) for i in range(8)]

            x_loaded = [sem(f"x1_loaded{i}") for i in range(CB)]
            consts = sem("consts")
            watt_turned = sem("watt_turned")
            watt_t_ready = sem("watt_t_ready")
            a1wide_ready = sem("a1wide_ready")
            wa_done = sem("wa_done")
            wa_ready = sem("wa_ready")
            deg_chain = sem("deg_chain")
            z_loaded = [sem(f"z_loaded{i}") for i in range(2)]
            projected = sem("projected")
            x1_part = sem("x1_part")
            x1_ready = sem("x1_ready")
            stats_chain = sem("stats_chain")
            factors_chain = sem("factors_chain")
            stats_ready = sem("stats1_ready")
            sqrt_done = sem("sqrt1_done")
            factors_ready = sem("factors1_ready")
            hn_ready = sem("hn_ready")
            hn_turned = sem("hn_turned")
            hn_t_ready = sem("hn_t_ready")
            h_done = sem("h_done")
            h_saved = sem("h_saved")
            sum_done = sem("sum_done")
            top_chain = sem("top_chain")
            top_turned = sem("top_turned")
            top_spread = sem("top_spread")
            mean_done = sem("mean_done")
            w_ready = sem("w_ready")
            v_ready = sem("v_ready")
            hv_ready = sem("hv_ready")
            c_raw = sem("c_raw")
            c_ready = sem("c_ready")
            m_loaded = [sem(f"m_loaded{i}") for i in range(2)]
            r_ready = sem("r_ready")
            p_ready = sem("p_ready")
            p_used = sem("p_used")
            acc_free = sem("acc_free")
            evac_chain = sem("evac_chain")
            y_ready = sem("y_ready")
            y_stored = [sem(f"y_stored{i}") for i in range(2)]
            y_free = sem("y_free")
            R_SLOTS, P_SLOTS = 2, 4
            TURN_LAG, ATTEND_LAG = 4, 5
            PEELED = 6
            assert PEELED % 2 == 0 and PEELED > ATTEND_LAG

            block = ctx.enter_context(nc.Block("layer1"))

            @block.sync
            def _(sp):
                for c in range(CB):
                    sp.dma_start(x1[:, bass.ts(c, LNT), :], x_rows[c]).then_inc(x_loaded[c], 16)

                def load_z(c, par):
                    sp.dma_start(z_in[:, par, :], in_sum[:, bass.ts(c, ROWS)]).then_inc(z_loaded[par], 16)
                    sp.dma_start(z_out[:, par, :], out_sum[:, bass.ts(c, ROWS)]).then_inc(z_loaded[par], 16)

                for par in range(2):
                    load_z(PEELED + par, par)
                with sp.Fori(PEELED // 2 + 1, IB // 2) as g:
                    for par in range(2):
                        wait_alone(sp, projected, 2 * g + par - 1)
                        load_z(2 * g + par, par)

                def load_mask(b, chunk, s):
                    sp.dma_start(m_tile[:, s, :, :], mask_dram[b, :, bass.ds(chunk * CH, CH), :]) \
                        .then_inc(m_loaded[s], 16)

                load_mask(0, 0, 0)
                load_mask(0, 1, 1)
                with sp.Fori(1, IB * CHUNKS // 2) as g:
                    for s in range(2):
                        n = 2 * g + s
                        wait_alone(sp, p_ready, R_SLOTS + CSUB * (n - 1))
                        load_mask(n // CHUNKS, n & (CHUNKS - 1), s)

            @block.tensor
            def _(pe):
                def project(c, par, rows_in, rows_out):
                    pe.wait_ge(x1_ready, c + 1)
                    for t in range(IT):
                        pe.matmul(bank[par][:, bass.ts(t, D)], rows_in[:, bass.ts(t, P)], win[:, :],
                                  start=True, stop=True)
                        ins = pe.matmul(bank[2 + par][:, bass.ts(t, D)], rows_out[:, bass.ts(t, P)], wout[:, :],
                                        start=True, stop=True)
                    ins.then_inc(projected, 1)

                def turn_hn(c, par):
                    pe.wait_ge(hn_ready, 2 + c + 1)
                    for t in range(IT):
                        ins = pe.transpose(bank[4][:, bass.ts(t, P)], hn[:, par, bass.ts(t, P)], ident[:, :])
                    ins.then_inc(hn_turned, 1)

                def attend_inputs(c, par):
                    pe.wait_ge(hn_t_ready, c + 1)
                    pe.wait_ge(h_saved, c + 1)
                    pe.matmul(bank[5][:, 0:ROWS], wa1[:, :], hn_t[:, par, :], start=True, stop=True)
                    for t in range(IT):
                        ins = pe.matmul(bank[6 + t // 2][:, bass.ts(t % 2, DE)], hn_t[:, par, bass.ts(t, P)],
                                        watt[:, :], start=True, stop=True)
                    ins.then_inc(h_done, 1)

                def attend_weights():
                    pe.transpose(bank[5][:, 0:D], watt[:, 0:D], ident[:, :]).then_inc(watt_turned, 1)
                    pe.wait_ge(watt_t_ready, 1)
                    pe.wait_ge(a1wide_ready, 1)
                    pe.matmul(bank[6][:, 0:P], watt_t[:, :], a1wide[:, :], start=True, stop=True)
                    pe.matmul(bank[7][:, 0:1], watt_t[:, :], a2col[:, :], start=True, stop=True).then_inc(wa_done, 1)
                    pe.wait_ge(wa_ready, 2)

                pe.wait_ge(weights_loaded, 16 * len(weights))
                for c in range(PEELED):
                    if c == 2:
                        attend_weights()
                    rows = bass.ts(c, ROWS)
                    project(c, c % 2, in_sum[:, rows], out_sum[:, rows])
                    if c >= ATTEND_LAG:
                        attend_inputs(c - ATTEND_LAG, (c - ATTEND_LAG) % 2)
                    if c >= TURN_LAG:
                        turn_hn(c - TURN_LAG, (c - TURN_LAG) % 2)
                with pe.Fori(PEELED // 2, IB // 2) as g:
                    for par in range(2):
                        c = 2 * g + par
                        pe.wait_ge(z_loaded[par], 32 * (g - PEELED // 2 + 1))
                        project(c, par, z_in[:, par, :], z_out[:, par, :])
                        attend_inputs(c - ATTEND_LAG, (par + ATTEND_LAG) % 2)
                        turn_hn(c - TURN_LAG, (par + TURN_LAG) % 2)
                for c in range(IB, IB + ATTEND_LAG):
                    attend_inputs(c - ATTEND_LAG, (c - ATTEND_LAG) % 2)
                    if c - TURN_LAG < IB:
                        turn_hn(c - TURN_LAG, (c - TURN_LAG) % 2)

                pe.wait_ge(top_chain, 1)
                pe.transpose(bank[0][0:1, 0:P], top_part[:, :], ident[:, :]).then_inc(top_turned, 1)
                pe.wait_ge(top_chain, 2)
                pe.matmul(bank[1][:, 0:1], ones[0:1, :], top_one[:, :], start=True, stop=True).then_inc(top_spread, 1)
                def mean_row():
                    pe.wait_ge(sum_done, IB + 1)
                    for t in range(IT):
                        ins = pe.matmul(bank[IT][:, 0:D], mean_w[:, :], h_sum[:, t, 0:D], start=(t == 0), stop=(t == IT - 1))
                    ins.then_inc(mean_done, 1)

                def chunk(b, ch, s, par, first):
                    for i in range(CSUB):
                        j = ch * CSUB + i
                        k = (s * CSUB + i) % P_SLOTS
                        pe.wait_ge(p_ready, R_SLOTS + b * SUBS + j + 1)
                        for half in range(2):
                            for t in range(IT):
                                ins = pe.matmul(bank[IT * par + t][:, 0:DE], p_tile[:, k, half, bass.ts(t, P)],
                                                hv[:, 2 * j + half, :],
                                                start=(first and i == 0 and half == 0), stop=(i == CSUB - 1 and half == 1),
                                                skip_group_check=True)
                        ins.then_inc(p_used, 1)

                def row_block(g, par, first=False):
                    b = 2 * g + par
                    pe.wait_ge(acc_free, b + 1)
                    for s in range(2):
                        pe.wait_ge(hv_ready, s + 1)
                        chunk(b, s, s, par, s == 0)
                    if first:
                        mean_row()
                    with pe.Fori(1, CHUNKS // 2) as cp:
                        for s in range(2):
                            pe.wait_ge(hv_ready, 2 * cp + s + 1)
                            chunk(b, 2 * cp + s, s, par, False)

                pe.wait_ge(top_chain, 3)
                row_block(0, 0, True)
                row_block(0, 1)
                with pe.Fori(1, IB // 2) as g:
                    for par in range(2):
                        row_block(g, par)

            @block.scalar
            def _(act):
                def normalise(g):
                    act.wait_ge(factors_ready, g + 1)
                    for t in range(LNT):
                        ins = nc.scalar.activation(hn[:, t // IT, bass.ts(t % IT, P)], x1[:, LNT * g + t, :], ACT.Relu,
                                                   bias=shift[:, t:t + 1], scale=rstd[:, t:t + 1])
                        if t % IT == IT - 1:
                            ins.then_inc(hn_ready, 1)

                def copy_turned(c, par):
                    act.wait_ge(hn_turned, c + 1)
                    nc.scalar.copy(hn_t[:, par, :], bank[4][:, :]).then_inc(hn_t_ready, 1)

                def save(c):
                    act.wait_ge(h_done, c + 1)
                    nc.scalar.copy(in_sum[:, bass.ts(c, ROWS)], bank[5][:, :])
                    for half in range(2):
                        ins = nc.scalar.copy(hv[:, bass.ds(c * IT + 2 * half, 2), :],
                                             bank[6 + half][:, 0:2 * DE].rearrange("p (t d) -> p t d", d=DE))
                    ins.then_inc(h_saved, 1)

                act.wait_ge(watt_turned, 1)
                nc.scalar.copy(watt_t[:, :], bank[5][:, 0:D]).then_inc(watt_t_ready, 1)
                act.wait_ge(wa_done, 1)
                nc.scalar.copy(wa1[:, :], bank[6][:, 0:P]).then_inc(wa_ready, 1)
                nc.scalar.copy(watt[:, D:DE], bank[7][:, 0:1]).then_inc(wa_ready, 1)
                norm_root(act, 0, stats_ready, sqrt_done)
                normalise(0)
                norm_root(act, 1, stats_ready, sqrt_done)
                copy_turned(0, 0)
                save(0)
                copy_turned(1, 1)
                with act.Fori(PEELED // 2, IB // 2) as g:
                    for par in range(2):
                        c = 2 * g + par
                        if par == 0:
                            normalise(g - TURN_LAG // 2)
                            norm_root(act, g - 1, stats_ready, sqrt_done)
                        save(c - ATTEND_LAG)
                        copy_turned(c - TURN_LAG, par)
                for c in range(IB, IB + ATTEND_LAG):
                    if c - TURN_LAG < IB and c % 2 == 0:
                        normalise((c - TURN_LAG) // 2)
                    if c == IB:
                        norm_root(act, IB // 2 - 1, stats_ready, sqrt_done)
                    if c == IB + ATTEND_LAG - 1:
                        nc.scalar.activation(table_probe[:, :], eps[:, :], ACT.Exp)
                    save(c - ATTEND_LAG)
                    if c - TURN_LAG < IB:
                        copy_turned(c - TURN_LAG, c % 2)

                s2 = hv[:, :, D]
                act.wait_ge(top_chain, 6)
                nc.scalar.activation(w_col[:, :], s2, ACT.Exp, bias=w_bias[:, 0:1], scale=1 - SLOPE).then_inc(w_ready, 1)
                nc.scalar.activation(v_col[:, :], s2, ACT.Exp, bias=v_bias[:, 0:1], scale=SLOPE).then_inc(v_ready, 1)

                def c_of(b, par):
                    nc.scalar.activation(c_row[:, par, :], in_sum[:, bass.ts(b, ROWS)], ACT.Exp,
                                         bias=c_bias[:, 0:1], scale=1 - SLOPE).then_inc(c_raw, 1)

                def chunk(b, ch, s, par):
                    for i in range(CSUB):
                        j = ch * CSUB + i
                        act.wait_ge(p_ready, b * SUBS + j + 1)
                        for half in range(2):
                            ins = nc.scalar.activation(r_tile[:, i % 2, half, :], c_row[:, par, :], ACT.Relu,
                                                       bias=minus1[:, 0:1], scale=w_col[:, bass.ds(2 * j + half, 1)])
                        ins.then_inc(r_ready, 1)

                c_of(0, 0)
                act.wait_ge(w_ready, 1)
                with act.Fori(0, IB // 2) as g:
                    for par in range(2):
                        b = 2 * g + par
                        act.wait_ge(c_ready, b + 1)
                        chunk(b, 0, 0, par)
                        c_of((b + 1) & (IB - 1), 1 - par)
                        with act.Fori(1, CHUNKS) as ch:
                            chunk(b, ch, 0, par)

            @block.vector
            def _(dve):
                dve.memset(minus1[:, :], -1.0)
                dve.memset(ones[:, :], 1.0)
                dve.memset(mean_w[:, :], 1.0 / N).then_inc(consts, 1)
                dve.sem_inc(x1_ready, 2)
                dve.sem_inc(hn_ready, 2)
                dve.sem_inc(h_saved, 1)
                dve.sem_inc(y_free, 2)
                dve.sem_inc(p_ready, R_SLOTS)
                dve.sem_inc(acc_free, 1)

                dve.wait_ge(consts, 1)
                dve.wait_ge(weights_loaded, 16 * len(weights))
                dve.tensor_scalar(a1wide[:, :], ones[:, :], a1col[:, 0:1], None, ALU.mult).then_inc(a1wide_ready, 1)

                dve.tensor_reduce(degree[:, 0, :], row_parts[:, :, :], AX_X, ALU.add)
                dve.tensor_reduce(degree[:, 1, :], col_parts[:, :, :], AX_X, ALU.add).then_inc(deg_chain, 1)
                dve.wait_ge(deg_chain, 1)
                dve.tensor_scalar(positive[:, :, :], degree[:, :, :], 0.0, None, ALU.is_gt).then_inc(deg_chain, 1)
                dve.wait_ge(deg_chain, 2)
                dve.tensor_tensor(guarded[:, :, :], degree[:, :, :], positive[:, :, :], ALU.mult).then_inc(deg_chain, 1)
                dve.wait_ge(deg_chain, 3)
                dve.scalar_tensor_tensor(out=guarded[:, :, :].rearrange("p a b -> p (a b)"),
                                         in0=guarded[:, :, :].rearrange("p a b -> p (a b)"), scalar=1.0,
                                         in1=positive[:, :, :].rearrange("p a b -> p (a b)"),
                                         op0=ALU.add, op1=ALU.subtract).then_inc(deg_chain, 1)
                dve.wait_ge(deg_chain, 4)
                dve.reciprocal(inverse[:, :, :], guarded[:, :, :]).then_inc(deg_chain, 1)
                dve.wait_ge(deg_chain, 5)

                def add_share(c, par, direction, done):
                    for t in range(IT):
                        row = x1[:, c * IT + t, :]
                        ins = dve.scalar_tensor_tensor(out=row, in0=bank[2 * direction + par][:, bass.ts(t, D)],
                                                       scalar=inverse[:, direction, bass.ds(c * IT + t, 1)], in1=row,
                                                       op0=ALU.mult, op1=ALU.add)
                    ins.then_inc(done, 1)

                def residual(g):
                    for par in range(2):
                        dve.wait_ge(projected, 2 * g + par + 1)
                        add_share(2 * g + par, par, 0, x1_part)
                    for par in range(2):
                        dve.wait_ge(x1_part, 2 * g + par + 1)
                        add_share(2 * g + par, par, 1, x1_ready)

                def factors(g, first=False):
                    wait_alone(dve, x1_ready, 2 + 2 * g + 2)
                    norm_stats(dve, lambda t: x1[:, 2 * g * IT + t, :], stats_chain, g, stats_ready)
                    if not first:
                        dve.wait_ge(hn_ready, 2 + 2 * g)
                    dve.wait_ge(sqrt_done, g + 1)
                    norm_factors(dve, factors_chain, FACTORS_CHAIN * g, factors_ready)

                for g in range(PEELED // 2):
                    dve.wait_ge(x_loaded[g], 16)
                    residual(g)
                    factors(g, g == 0)
                for c in range(PEELED // 2, CB):
                    dve.wait_ge(x_loaded[c], 16)
                with dve.Fori(PEELED // 2, IB // 2) as g:
                    residual(g)
                    factors(g)

                dve.wait_ge(h_saved, 1 + IB)
                dve.tensor_reduce(top_part[:, :], hv[:, :, D], AX_X, ALU.max).then_inc(top_chain, 1)
                dve.wait_ge(top_turned, 1)
                dve.tensor_reduce(top_one[:, :], bank[0][0:1, 0:P], AX_X, ALU.max).then_inc(top_chain, 1)
                dve.wait_ge(top_spread, 1)
                dve.tensor_copy(top[:, :], bank[1][:, 0:1]).then_inc(top_chain, 1)
                dve.wait_ge(top_chain, 3)
                dve.tensor_scalar(w_bias[:, :], top[:, :], SLOPE - 1, None, ALU.mult)
                dve.tensor_scalar(v_bias[:, :], top[:, :], -SLOPE, None, ALU.mult).then_inc(top_chain, 1)
                dve.tensor_tensor(top_b[:, :], top[:, :], bias[:, :], ALU.add).then_inc(top_chain, 1)
                dve.wait_ge(top_chain, 5)
                dve.tensor_scalar(c_bias[:, :], top_b[:, :], 1 - SLOPE, None, ALU.mult).then_inc(top_chain, 1)

                def cap(b, par):
                    dve.wait_ge(c_raw, b + 1)
                    dve.tensor_scalar(c_row[:, par, :], c_row[:, par, :], CAP, None, ALU.min).then_inc(c_ready, 1)

                def chunk(b, ch, s):
                    for i in range(CSUB):
                        q = b * SUBS + ch * CSUB + i
                        k = (s * CSUB + i) % P_SLOTS
                        dve.wait_ge(r_ready, q + 1)
                        dve.wait_ge(p_used, q + 1)
                        dve.scalar_tensor_tensor(out=p_tile[:, k, :, :].rearrange("p a b -> p (a b)"),
                                                 in0=r_tile[:, i % 2, :, :].rearrange("p a b -> p (a b)"), scalar=1.0,
                                                 in1=m_tile[:, s, 2 * i:2 * i + 2, :].rearrange("p a b -> p (a b)"),
                                                 op0=ALU.add, op1=ALU.mult).then_inc(p_ready, 1)

                EVAC = 3

                def finish(b, par):
                    dve.wait_ge(p_used, P_SLOTS + SUBS * (b + 1))
                    for t in range(IT):
                        ins = dve.tensor_scalar(empty[:, t:t + 1], bank[IT * par + t][:, D:DE], 0.0, None, ALU.is_equal)
                    ins.then_inc(evac_chain, 1)
                    dve.wait_ge(evac_chain, EVAC * b + 1)
                    for t in range(IT):
                        ins = dve.tensor_tensor(denom[:, t:t + 1], bank[IT * par + t][:, D:DE], empty[:, t:t + 1], ALU.add)
                    ins.then_inc(evac_chain, 1)
                    dve.wait_ge(evac_chain, EVAC * b + 2)
                    dve.reciprocal(invden[:, :], denom[:, :]).then_inc(evac_chain, 1)
                    dve.wait_ge(evac_chain, EVAC * b + 3)
                    dve.wait_ge(y_free, b + 1)
                    for t in range(IT):
                        ins = dve.scalar_tensor_tensor(out=y[:, par, t, :], in0=bank[IT * par + t][:, 0:D],
                                                       scalar=invden[:, t:t + 1], in1=x1[:, b * IT + t, :],
                                                       op0=ALU.mult, op1=ALU.add)
                    ins.then_inc(acc_free, 1)
                    dve.wait_ge(acc_free, 2 + b + 1)
                    for t in range(IT):
                        ins = dve.scalar_tensor_tensor(out=y[:, par, t, :], in0=h_mean[:, :], scalar=empty[:, t:t + 1],
                                                       in1=y[:, par, t, :], op0=ALU.mult, op1=ALU.add)
                    ins.then_inc(y_ready, 1)

                def row_block(g, par, first):
                    b = 2 * g + par
                    for s in range(2):
                        dve.wait_ge(m_loaded[s], 16 * (b * CHUNKS // 2 + 1))
                        chunk(b, s, s)
                    cap(b + 1, 1 - par)
                    if not first:
                        finish(b - 1, 1 - par)
                    with dve.Fori(1, CHUNKS // 2) as cp:
                        for s in range(2):
                            dve.wait_ge(m_loaded[s], 16 * (b * CHUNKS // 2 + cp + 1))
                            chunk(b, 2 * cp + s, s)

                cap(0, 0)
                row_block(0, 0, True)
                dve.wait_ge(mean_done, 1)
                dve.tensor_copy(h_mean[:, :], bank[IT][:, 0:D]).then_inc(acc_free, 1)
                row_block(0, 1, False)
                with dve.Fori(1, IB // 2) as g:
                    for par in range(2):
                        row_block(g, par, False)
                finish(IB - 1, 1)

            @block.gpsimd
            def _(pool):
                pool.sem_inc(p_used, P_SLOTS)
                nc.gpsimd.memset(h_sum[:, :, :], 0.0).then_inc(sum_done, 1)

                def add_h(c):
                    pool.wait_ge(h_saved, 1 + c + 1)
                    wait_alone(pool, sum_done, c + 1)
                    nc.gpsimd.tensor_tensor(h_sum[:, :, :], h_sum[:, :, :], hv[:, bass.ds(c * IT, IT), :],
                                            ALU.add).then_inc(sum_done, 1)

                with pool.Fori(0, IB - 1) as c:
                    add_h(c)

                pool.wait_ge(v_ready, 1)
                for ch in range(CHUNKS):
                    if ch == 1:
                        add_h(IB - 1)
                    if ch == CHUNKS - 1:
                        pool.wait_ge(sum_done, IB + 1)
                    at = slice(ch * CH, ch * CH + CH)
                    v = v_col[:, at].rearrange("p (t o) -> p t o", o=1)
                    nc.gpsimd.tensor_tensor(hv[:, at, 0:D], hv[:, at, 0:D], v.broadcast_to([P, CH, D]), ALU.mult)
                    nc.gpsimd.tensor_copy(hv[:, at, D:DE], v).then_inc(hv_ready, 1)

                def store(g, par):
                    b = 2 * g + par
                    pool.wait_ge(y_ready, b + 1)
                    pool.dma_start(out_rows[b], y[:, par, :, :]).then_inc(y_stored[par], 16)
                    pool.wait_ge(y_stored[par], 16 * (g + 1))
                    pool.sem_inc(y_free, 1)

                with pool.Fori(0, IB // 2) as g:
                    for par in range(2):
                        store(g, par)


_INS = ["x", "adj", "L0_gnn_W_in", "L0_gnn_W_out", "L1_gnn_W", "L1_gnn_a1", "L1_gnn_a2", "L1_gnn_a_bias"]


def kernel(**inputs):
    import numpy as _np
    import concourse.bacc as _bacc
    from concourse import mybir as _mybir
    from concourse.bass_utils import run_bass_kernel_spmd as _run

    nc = _bacc.Bacc("TRN2", target_bir_lowering=False, num_devices=1)
    arrays, args = {}, []
    for name in _INS:
        a = _np.ascontiguousarray(inputs[name])
        arrays[f"in_{name}_dram"] = a
        args.append(nc.dram_tensor(f"in_{name}_dram", a.shape, _mybir.dt.from_np(a.dtype), kind="ExternalInput").ap())
    out = nc.dram_tensor("out_0_dram", inputs["x"].shape, _mybir.dt.float32, kind="ExternalOutput").ap()
    graph_layers(nc, *args, out)
    r = _run(nc, [arrays], core_ids=[0])
    return r.results[0]["out_0_dram"]
```

```python
from contextlib import ExitStack

import concourse.bass as bass
from concourse import mybir

F32 = mybir.dt.float32
F32R = mybir.dt.float32r
U8 = mybir.dt.uint8
ALU = mybir.AluOpType
ACT = mybir.ActivationFunctionType
AX_X = mybir.AxisListType.X

P = 128
EPS = 1e-5
SLOPE = 0.2
CAP = float(2.0 ** 90)


def graph_layers(nc, x, adj, w_in, w_out, w_att, a1, a2, a_bias, out):
    N, D = x.shape
    assert D == P
    NT = N // P
    IT = 4
    ROWS = IT * P
    IB = N // ROWS
    JT = 8
    COLS = JT * P
    CB = N // COLS
    STEPS = CB * IB
    SUB = JT // 2
    LNT = 8
    assert SUB == IT and CB * LNT == NT and IB == 2 * CB

    x_rows = x.rearrange("(c t p) d -> c p t d", p=P, t=LNT)
    adj_v = adj.rearrange("(b t p) (c w) -> b c p t w", t=IT, p=P, w=COLS)
    mask_dram = nc.dram_tensor("mask_scratch", (IB, P, NT, ROWS), U8, kind="Internal").ap()
    out_rows = out.rearrange("(b t p) d -> b p t d", t=IT, p=P)

    with ExitStack() as whole:
        def keep(name, shape, dt=F32):
            return whole.enter_context(nc.sbuf_tensor(name, shape, dt))

        in_sum = keep("in_sum", [P, N])
        out_sum = keep("out_sum", [P, N])
        row_parts = keep("row_parts", [P, NT, CB])
        col_parts = keep("col_parts", [P, NT, IB])
        mask = keep("mask", [P, 2, JT, ROWS], U8)
        ident = keep("ident", [P, P])
        table_probe = keep("table_probe", [P, 1])
        eps = keep("eps", [P, 1])
        stats = keep("stats", [P, LNT, 6])
        moments = keep("moments", [P, LNT, 2])
        std = keep("std", [P, LNT])
        rstd0 = keep("rstd0", [P, LNT])
        newton = keep("newton", [P, LNT])
        rstd = keep("rstd", [P, LNT])
        shift = keep("shift", [P, LNT])
        win = keep("win", [P, D])
        wout = keep("wout", [P, D])
        watt = keep("watt", [P, D + 1])
        a1col = keep("a1col", [P, 1])
        a2col = keep("a2col", [P, 1])
        bias = keep("bias", [P, 1])

        mask_stored = [whole.enter_context(nc.semaphore(f"mask_stored{i}")) for i in range(2)]
        MASK_CREDIT = 16
        weights_loaded = whole.enter_context(nc.semaphore("weights_loaded"))
        waits_done = whole.enter_context(nc.semaphore("waits_done"))

        def wait_alone(eng, sem, value):
            eng.wait_ge(sem, value)
            eng.sem_inc(waits_done, 1)

        STATS_CHAIN, FACTORS_CHAIN = 2, 5

        def norm_stats(dve, row_tile, chain, before, stats_ready, half_ready=None):
            HALF = LNT // 2
            for t in range(LNT):
                if half_ready and t % HALF == 0:
                    half_ready(t // HALF)
                ins = dve.bn_stats(stats[:, t, :], row_tile(t))
                if t % HALF == HALF - 1:
                    ins.then_inc(chain, 1)
            for t in range(LNT):
                if t % HALF == 0:
                    wait_alone(dve, chain, before + t // HALF + 1)
                ins = dve.bn_aggr(moments[:, t, :], stats[:, t, :])
            ins.then_inc(stats_ready, 1)

        def norm_root(act, c, stats_ready, sqrt_done):
            act.wait_ge(stats_ready, c + 1)
            nc.scalar.activation(std[:, :], moments[:, :, 1], ACT.Sqrt, bias=eps[:, 0:1]).then_inc(sqrt_done, 1)

        def norm_factors(dve, chain, before, factors_ready):
            dve.reciprocal(rstd0[:, :], std[:, :]).then_inc(chain, 1)
            dve.wait_ge(chain, before + 1)
            dve.tensor_tensor(newton[:, :], rstd0[:, :], rstd0[:, :], ALU.mult).then_inc(chain, 1)
            dve.wait_ge(chain, before + 2)
            dve.scalar_tensor_tensor(out=newton[:, :], in0=moments[:, :, 1], scalar=EPS,
                                     in1=newton[:, :], op0=ALU.add, op1=ALU.mult).then_inc(chain, 1)
            dve.wait_ge(chain, before + 3)
            dve.tensor_scalar(newton[:, :], newton[:, :], -0.5, 1.5, ALU.mult, ALU.add).then_inc(chain, 1)
            dve.wait_ge(chain, before + 4)
            dve.tensor_tensor(rstd[:, :], rstd0[:, :], newton[:, :], ALU.mult).then_inc(chain, 1)
            dve.wait_ge(chain, before + 5)
            dve.scalar_tensor_tensor(out=shift[:, :], in0=moments[:, :, 0], scalar=-1.0,
                                     in1=rstd[:, :], op0=ALU.mult, op1=ALU.mult).then_inc(factors_ready, 1)

        with ExitStack() as ctx:
            def sb(name, shape, dt=F32):
                return ctx.enter_context(nc.sbuf_tensor(name, shape, dt))

            def sem(name):
                return ctx.enter_context(nc.semaphore(name))

            h0 = sb("h0", [P, N])
            a_tile = sb("a_tile", [P, 2, IT, COLS])
            lie_hi = sb("lie_hi", [P, 2, COLS], F32R)
            lie_lo = sb("lie_lo", [P, 2, COLS], F32R)
            turn_hi = sb("turn_hi", [P, 2, 2, ROWS], F32R)
            turn_lo = sb("turn_lo", [P, 2, 2, ROWS], F32R)
            rowh_hi = sb("rowh_hi", [P, 2, ROWS], F32R)
            rowh_lo = sb("rowh_lo", [P, 2, ROWS], F32R)
            colh_hi = sb("colh_hi", [P, COLS], F32R)
            colh_lo = sb("colh_lo", [P, COLS], F32R)
            turned = ctx.enter_context(nc.psum_tensor("turned", [P, 2, 2, ROWS], F32))
            acc_in = ctx.enter_context(nc.psum_tensor("acc_in", [P, 2, ROWS], F32))
            acc_out = ctx.enter_context(nc.psum_tensor("acc_out", [P, 2, COLS // 2], F32))

            TURN_SLOTS = LIE_SLOTS = ACC_SLOTS = 2
            LIE_CREDIT = 2 * SUB
            NORM_STATS, NORM_ROOT, NORM_FACTORS = (0, 1), (0, 3), (0, 4)
            NORM_TILES = {(0, 6): (0, 1), (1, 0): (2, 3), (1, 2): (4, 5), (1, 4): (6, 7)}
            ORDER = [(True, 0), (True, 1), (False, 0), (False, 1), (True, 2), (False, 2), (True, 3), (False, 3)]
            x_loaded = [sem(f"x_loaded{c}") for c in range(CB)]
            a_loaded = [sem(f"a_loaded{i}") for i in range(2)]
            ident_zero = sem("ident_zero")
            ident_ready = sem("ident_ready")
            eps_ready = sem("eps_ready")
            sum_cleared = sem("sum_cleared")
            ln_chain = sem("ln_chain")
            stats_ready = sem("stats_ready")
            sqrt_done = sem("sqrt_done")
            factors_ready = sem("factors_ready")
            h0_ready = sem("h0_ready")
            rowh_hi_done = sem("rowh_hi_done")
            rowh_ready = sem("rowh_ready")
            colh_hi_done = sem("colh_hi_done")
            colh_ready = sem("colh_ready")
            turned_done = sem("turned_done")
            turn_hi_done = sem("turn_hi_done")
            turn_ready = sem("turn_ready")
            turn_used = sem("turn_used")
            mask_done = sem("mask_done")
            lie_hi_done = sem("lie_hi_done")
            lie_ready = sem("lie_ready")
            lie_used = sem("lie_used")
            in_added = sem("in_added")
            out_saved = sem("out_saved")

            weights = ((watt[:, 0:D], w_att),
                       (a1col[:, :], a1.rearrange("(d o) -> d o", o=1)),
                       (a2col[:, :], a2.rearrange("(d o) -> d o", o=1)),
                       (win[:, :], w_in), (wout[:, :], w_out),
                       (bias[:, :], a_bias.rearrange("(a o) -> a o", o=1).broadcast_to([P, 1])))

            block = ctx.enter_context(nc.Block("layer0"))

            @block.sync
            def _(sp):
                def load(b, c, par):
                    sp.dma_start(a_tile[:, par, :, :], adj_v[b, c]).then_inc(a_loaded[par], 16)

                def store_mask(n, b, c, par):
                    wait_alone(sp, mask_done, TURN_SLOTS + SUB * (n + 1))
                    sp.dma_start(mask_dram[b, :, bass.ds(c * JT, JT), :], mask[:, par, :, :]) \
                        .then_inc(mask_stored[par], 16)

                def load_x(c):
                    sp.dma_start(out_sum[:, bass.ts(c, LNT * P)].rearrange("p (t d) -> p t d", d=P), x_rows[c]) \
                        .then_inc(x_loaded[c], 16)

                load_x(0)
                load(0, 0, 0)
                load_x(1)
                load(1, 0, 1)
                for c in range(2, CB):
                    load_x(c)
                for dst, src in weights:
                    sp.dma_start(dst, src).then_inc(weights_loaded, 16)
                with sp.Fori(1, STEPS // 2) as g:
                    for par in range(2):
                        n = 2 * g + par
                        sp.wait_ge(turned_done, SUB * (n - 1))
                        wait_alone(sp, lie_ready, SUB * (n - 1))
                        load(n & (IB - 1), n // IB, par)
                        store_mask(n - 2, (n - 2) & (IB - 1), (n - 2) // IB, par)
                for par in range(2):
                    store_mask(STEPS - 2 + par, IB - 2 + par, CB - 1, par)

            @block.tensor
            def _(pe):
                def turn(n, u, par):
                    m = SUB * n + u
                    pe.wait_ge(turn_ready, m + 1)
                    for k in range(2):
                        for t in range(IT):
                            ins = pe.transpose(turned[:, u % 2, k, bass.ts(t, P)],
                                               a_tile[:, par, t, bass.ts(2 * u + k, P)], ident[:, :])
                    ins.then_inc(turned_done, 1)

                def lying_product(n, u, par, first):
                    pe.wait_ge(lie_ready, SUB * n + u + 1)
                    hi, lo = (h[:, par, bass.ts(u, P)] for h in (rowh_hi, rowh_lo))
                    s = u % 2
                    for i, (h, a) in enumerate(((hi, lie_hi), (hi, lie_lo), (lo, lie_hi))):
                        for half in range(2):
                            ins = pe.matmul(acc_out[:, half, :], h, a[:, s, bass.ts(half, COLS // 2)],
                                            start=(first and u == 0 and i == 0), stop=(i == 2),
                                            skip_group_check=True)
                    ins.then_inc(lie_used, 1)

                def turned_product(n, u, par, c):
                    pe.wait_ge(turn_ready, TURN_SLOTS + SUB * n + u + 1)
                    pe.wait_ge(colh_ready, SUB * c + u + 1)
                    s = u % 2
                    for k in range(2):
                        hi, lo = (h[:, bass.ts(2 * u + k, P)] for h in (colh_hi, colh_lo))
                        for i, (h, a) in enumerate(((hi, turn_hi), (hi, turn_lo), (lo, turn_hi))):
                            ins = pe.matmul(acc_in[:, par, :], h, a[:, s, k, :],
                                            start=(u == 0 and k == 0 and i == 0),
                                            stop=(u == SUB - 1 and k == 1 and i == 2))
                    ins.then_inc(turn_used, 1)

                def pair(c, p, first):
                    for par in range(2):
                        n = IB * c + 2 * p + par
                        new = first and par == 0
                        pe.wait_ge(a_loaded[par], 16 * ((IB // 2) * c + p + 1))
                        turn(n, 0, par)
                        pe.wait_ge(rowh_ready, n + 1)
                        if new:
                            pe.wait_ge(out_saved, c + 1)
                        lying_product(n, 0, par, new)
                        turn(n, 1, par)
                        lying_product(n, 1, par, False)
                        pe.wait_ge(in_added, n + 1)
                        turned_product(n, 0, par, c)
                        turn(n, 2, par)
                        turned_product(n, 1, par, c)
                        turn(n, 3, par)
                        for u in range(2, SUB):
                            lying_product(n, u, par, False)
                            turned_product(n, u, par, c)

                pe.wait_ge(ident_ready, 1)
                with pe.Fori(0, CB) as c:
                    pair(c, 0, True)
                    with pe.Fori(1, IB // 2) as p:
                        pair(c, p, False)

            @block.scalar
            def _(act):
                act.wait_ge(eps_ready, 1)
                nc.scalar.activation(table_probe[:, :], eps[:, :], ACT.Sqrt)

                def normalise(c, tiles):
                    act.wait_ge(factors_ready, c + 1)
                    for t in tiles:
                        at = bass.ds((c * LNT + t) * P, P)
                        ins = nc.scalar.activation(h0[:, at], out_sum[:, at], ACT.Relu,
                                                   bias=shift[:, t:t + 1], scale=rstd[:, t:t + 1])
                        if t % IT == IT - 1:
                            ins.then_inc(h0_ready, 1)

                def save_out(c):
                    act.wait_ge(lie_used, LIE_CREDIT + SUB * IB * (c + 1))
                    nc.scalar.copy(out_sum[:, bass.ts(c, COLS)], acc_out[:, :, :].rearrange("p a b -> p (a b)")) \
                        .then_inc(out_saved, 1)

                def copy_in(n, b, par):
                    act.wait_ge(turn_used, TURN_SLOTS + SUB * (n + 1))
                    nc.scalar.copy(in_sum[:, bass.ts(b, ROWS)], acc_in[:, par, :]).then_inc(in_added, 1)

                def pair(c, p, norm=None, copies=False, first=False, save=None):
                    for par in range(2):
                        n = IB * c + 2 * p + par
                        b = 2 * p + par
                        act.wait_ge(a_loaded[par], 16 * ((IB // 2) * c + p + 1))
                        for item, (lying, u) in enumerate(ORDER):
                            if norm is not None and (par, item) == NORM_ROOT:
                                norm_root(act, norm, stats_ready, sqrt_done)
                            if norm is not None and (par, item) in NORM_TILES:
                                normalise(norm, NORM_TILES[par, item])
                            m = SUB * n + u
                            s = u % 2
                            if lying:
                                act.wait_ge(lie_used, m + LIE_CREDIT - LIE_SLOTS + 1)
                                nc.scalar.activation(lie_hi[:, s, :], a_tile[:, par, u, :], ACT.Copy,
                                                     accum_out=row_parts[:, b * IT + u, bass.ds(c, 1)]) \
                                    .then_inc(lie_hi_done, 1)
                                if save is not None and (par, item) == (0, 0):
                                    save_out(save)
                                if first and (par, item) == (0, 0):
                                    normalise(0, range(IT, LNT))
                                continue
                            act.wait_ge(turned_done, m + 1)
                            act.wait_ge(turn_used, m + 1)
                            act.wait_ge(mask_done, m + 1)
                            for k in range(2):
                                ins = nc.scalar.activation(
                                    turn_hi[:, s, k, :], turned[:, s, k, :], ACT.Copy,
                                    accum_out=col_parts[:, c * JT + 2 * u + k, bass.ds(b, 1)])
                            ins.then_inc(turn_hi_done, 1)
                            if copies and u == 1 and not (first and par == 0):
                                copy_in(n - 1, b - 1, 1 - par)

                norm_root(act, 0, stats_ready, sqrt_done)
                normalise(0, range(IT))
                pair(0, 0, norm=1, copies=True, first=True)
                with act.Fori(1, CB - 1) as p:
                    pair(0, p, norm=p + 1, copies=True)
                pair(0, CB - 1, copies=True)
                with act.Fori(1, CB) as c:
                    pair(c, 0, save=c - 1)
                    with act.Fori(1, IB // 2) as p:
                        pair(c, p)
                save_out(CB - 1)

            @block.vector
            def _(dve):
                dve.memset(eps[:, :], EPS).then_inc(eps_ready, 1)
                dve.sem_inc(turn_ready, TURN_SLOTS)
                dve.sem_inc(in_added, ACC_SLOTS)

                def layer_stats(c):
                    norm_stats(dve, lambda t: out_sum[:, bass.ds((c * LNT + t) * P, P)],
                               ln_chain, (STATS_CHAIN + FACTORS_CHAIN) * c, stats_ready)

                def layer_factors(c):
                    dve.wait_ge(sqrt_done, c + 1)
                    norm_factors(dve, ln_chain, (STATS_CHAIN + FACTORS_CHAIN) * c + STATS_CHAIN,
                                 factors_ready)

                def add_in(n, b, par):
                    dve.wait_ge(turn_used, TURN_SLOTS + SUB * (n + 1))
                    rows = in_sum[:, bass.ts(b, ROWS)]
                    dve.tensor_tensor(rows, acc_in[:, par, :], rows, ALU.add).then_inc(in_added, 1)

                def pair(c, p, norm=None, adds=True):
                    for par in range(2):
                        n = IB * c + 2 * p + par
                        for item, (lying, u) in enumerate(ORDER):
                            if norm is not None and (par, item) == NORM_STATS:
                                layer_stats(norm)
                            if norm is not None and (par, item) == NORM_FACTORS:
                                dve.wait_ge(h0_ready, 2 * norm)
                                layer_factors(norm)
                            m = SUB * n + u
                            s = u % 2
                            if lying:
                                dve.wait_ge(lie_hi_done, m + 1)
                                dve.tensor_tensor(lie_lo[:, s, :], a_tile[:, par, u, :],
                                                  lie_hi[:, s, :].bitcast(F32), ALU.subtract).then_inc(lie_ready, 1)
                                continue
                            dve.wait_ge(turn_hi_done, m + 1)
                            dve.tensor_tensor(turn_lo[:, s, :, :].rearrange("p a b -> p (a b)"),
                                              turned[:, s, :, :].rearrange("p a b -> p (a b)"),
                                              turn_hi[:, s, :, :].rearrange("p a b -> p (a b)").bitcast(F32),
                                              ALU.subtract).then_inc(turn_ready, 1)
                            if u == 0:
                                dve.wait_ge(mask_stored[par], MASK_CREDIT + 16 * ((IB // 2) * c + p))
                            dve.tensor_scalar(mask[:, par, 2 * u:2 * u + 2, :].rearrange("p a b -> p (a b)"),
                                              turn_hi[:, s, :, :].rearrange("p a b -> p (a b)").bitcast(F32),
                                              0.0, None, ALU.is_gt).then_inc(mask_done, 1)
                            if u == 1 and adds:
                                add_in(n - 1, (2 * p + par + IB - 1) & (IB - 1), 1 - par)

                dve.wait_ge(x_loaded[0], 16)
                layer_stats(0)
                layer_factors(0)
                dve.wait_ge(h0_ready, 1)
                dve.tensor_copy(rowh_hi[:, 0, :], h0[:, 0:ROWS]).then_inc(rowh_hi_done, 1)
                dve.wait_ge(rowh_hi_done, 1)
                dve.tensor_tensor(rowh_lo[:, 0, :], h0[:, 0:ROWS], rowh_hi[:, 0, :].bitcast(F32),
                                  ALU.subtract).then_inc(rowh_ready, 1)
                dve.wait_ge(x_loaded[1], 16)
                pair(0, 0, norm=1, adds=False)
                for c in range(2, CB):
                    dve.wait_ge(x_loaded[c], 16)
                with dve.Fori(1, CB - 1) as p:
                    pair(0, p, norm=p + 1, adds=False)
                pair(0, CB - 1, adds=False)
                dve.wait_ge(sum_cleared, 1)
                with dve.Fori(1, CB) as c:
                    with dve.Fori(0, IB // 2) as p:
                        pair(c, p)
                add_in(STEPS - 1, IB - 1, 1)

            @block.gpsimd
            def _(pool):
                pool.sem_inc(turn_used, TURN_SLOTS)
                pool.sem_inc(lie_used, LIE_CREDIT)
                pool.sem_inc(mask_done, TURN_SLOTS)
                pool.sem_inc(out_saved, 1)
                for par in range(2):
                    pool.sem_inc(mask_stored[par], MASK_CREDIT)
                nc.gpsimd.memset(ident[:, :], 0.0).then_inc(ident_zero, 1)
                pool.wait_ge(ident_zero, 1)
                nc.gpsimd.affine_select(out=ident[:, :], in_=ident[:, :], compare_op=ALU.not_equal, fill=1.0,
                                        base=0, pattern=[[-1, P]], channel_multiplier=1).then_inc(ident_ready, 1)
                nc.gpsimd.memset(in_sum[:, bass.ts(IB - 1, ROWS)], 0.0).then_inc(sum_cleared, 1)

                def split_rows(n, b, par):
                    pool.wait_ge(rowh_ready, 1)
                    pool.wait_ge(lie_used, LIE_CREDIT + SUB * (n - 1))
                    h = h0[:, bass.ts(b, ROWS)]
                    nc.gpsimd.tensor_copy(rowh_hi[:, par, :], h).then_inc(rowh_hi_done, 1)
                    wait_alone(pool, rowh_hi_done, n + 1)
                    nc.gpsimd.tensor_tensor(rowh_lo[:, par, :], h, rowh_hi[:, par, :].bitcast(F32),
                                            ALU.subtract).then_inc(rowh_ready, 1)

                def split_columns(c):
                    pool.wait_ge(turn_used, TURN_SLOTS + SUB * IB * c)
                    for u in range(SUB):
                        pool.wait_ge(h0_ready, 2 * c + u // 2 + 1)
                        at = bass.ts(u, COLS // SUB)
                        h = h0[:, bass.ds(c * COLS + u * (COLS // SUB), COLS // SUB)]
                        nc.gpsimd.tensor_copy(colh_hi[:, at], h).then_inc(colh_hi_done, 1)
                        wait_alone(pool, colh_hi_done, SUB * c + u + 1)
                        nc.gpsimd.tensor_tensor(colh_lo[:, at], h, colh_hi[:, at].bitcast(F32),
                                                ALU.subtract).then_inc(colh_ready, 1)

                with pool.Fori(0, CB) as c:
                    split_columns(c)
                    with pool.Fori(0, IB // 2) as p:
                        for par in range(2):
                            n = IB * c + 2 * p + par
                            b = (2 * p + par + 1) & (IB - 1)
                            pool.wait_ge(h0_ready, b + 1)
                            split_rows(n + 1, b, 1 - par)

        with ExitStack() as ctx:
            def sb(name, shape, dt=F32):
                return ctx.enter_context(nc.sbuf_tensor(name, shape, dt))

            def sem(name):
                return ctx.enter_context(nc.semaphore(name))

            DE = D + 1
            SUBS = NT // 2
            CH = JT
            CHUNKS = NT // CH
            CSUB = CH // 2

            x1 = sb("x1", [P, NT, D])
            hv = sb("hv", [P, NT, DE])
            watt_t = sb("watt_t", [P, D])
            a1wide = sb("a1wide", [P, P])
            wa1 = sb("wa1", [P, P])
            ones = sb("ones", [P, P])
            mean_w = sb("mean_w", [P, P])
            degree = sb("degree", [P, 2, NT])
            positive = sb("positive", [P, 2, NT])
            guarded = sb("guarded", [P, 2, NT])
            inverse = sb("inverse", [P, 2, NT])
            z_in = sb("z_in", [P, 2, ROWS])
            z_out = sb("z_out", [P, 2, ROWS])
            hn = sb("hn", [P, 2, ROWS])
            hn_t = sb("hn_t", [P, 2, ROWS])
            h_sum = sb("h_sum", [P, IT, DE])
            h_mean = sb("h_mean", [P, D])
            top_part = sb("top_part", [P, 1])
            top_one = sb("top_one", [1, 1])
            w_bias = sb("w_bias", [P, 1])
            v_bias = sb("v_bias", [P, 1])
            c_bias = sb("c_bias", [P, 1])
            minus1 = sb("minus1", [P, 1])
            w_col = sb("w_col", [P, NT])
            v_col = sb("v_col", [P, NT])
            c_row = sb("c_row", [P, 2, ROWS])
            r_tile = sb("r_tile", [P, 2, 2, ROWS])
            p_tile = sb("p_tile", [P, 4, 2, ROWS])
            empty = sb("empty", [P, IT])
            denom = sb("denom", [P, IT])
            invden = sb("invden", [P, IT])
            y = sb("y", [P, 2, IT, D])
            bank = [ctx.enter_context(nc.psum_tensor(f"bank{i}", [P, 512], F32)) for i in range(8)]

            x_loaded = [sem(f"x1_loaded{i}") for i in range(CB)]
            consts = sem("consts")
            watt_turned = sem("watt_turned")
            watt_t_ready = sem("watt_t_ready")
            a1wide_ready = sem("a1wide_ready")
            wa_done = sem("wa_done")
            wa_ready = sem("wa_ready")
            deg_chain = sem("deg_chain")
            z_loaded = [sem(f"z_loaded{i}") for i in range(2)]
            projected = sem("projected")
            x1_part = sem("x1_part")
            x1_ready = sem("x1_ready")
            stats_chain = sem("stats_chain")
            factors_chain = sem("factors_chain")
            stats_ready = sem("stats1_ready")
            sqrt_done = sem("sqrt1_done")
            factors_ready = sem("factors1_ready")
            hn_ready = sem("hn_ready")
            hn_turned = sem("hn_turned")
            hn_t_ready = sem("hn_t_ready")
            h_done = sem("h_done")
            h_saved = sem("h_saved")
            sum_done = sem("sum_done")
            top_chain = sem("top_chain")
            top_turned = sem("top_turned")
            top_spread = sem("top_spread")
            mean_done = sem("mean_done")
            w_ready = sem("w_ready")
            v_ready = sem("v_ready")
            hv_ready = sem("hv_ready")
            c_raw = sem("c_raw")
            c_ready = sem("c_ready")
            m_loaded = [sem(f"m_loaded{i}") for i in range(2)]
            r_ready = sem("r_ready")
            p_ready = sem("p_ready")
            p_used = sem("p_used")
            acc_free = sem("acc_free")
            evac_chain = sem("evac_chain")
            y_ready = sem("y_ready")
            y_stored = [sem(f"y_stored{i}") for i in range(2)]
            y_free = sem("y_free")
            last_stored = sem("last_stored")
            R_SLOTS, P_SLOTS = 2, 4
            TURN_LAG, ATTEND_LAG = 4, 5
            PEELED = 6
            assert PEELED % 2 == 0 and PEELED > ATTEND_LAG

            block = ctx.enter_context(nc.Block("layer1"))

            @block.sync
            def _(sp):
                for c in range(CB):
                    sp.dma_start(x1[:, bass.ts(c, LNT), :], x_rows[c]).then_inc(x_loaded[c], 16)

                def load_z(c, par):
                    sp.dma_start(z_in[:, par, :], in_sum[:, bass.ts(c, ROWS)]).then_inc(z_loaded[par], 16)
                    sp.dma_start(z_out[:, par, :], out_sum[:, bass.ts(c, ROWS)]).then_inc(z_loaded[par], 16)

                for par in range(2):
                    load_z(PEELED + par, par)
                with sp.Fori(PEELED // 2 + 1, IB // 2) as g:
                    for par in range(2):
                        wait_alone(sp, projected, 2 * g + par - 1)
                        load_z(2 * g + par, par)

                def load_mask(b, chunk, s):
                    sp.dma_start(mask[:, s, :, :], mask_dram[b, :, bass.ds(chunk * CH, CH), :]) \
                        .then_inc(m_loaded[s], 16)

                for s in range(2):
                    sp.wait_ge(mask_stored[s], MASK_CREDIT + 16 * (STEPS // 2))
                for s in range(2):
                    load_mask(0, s, s)
                with sp.Fori(1, IB * CHUNKS // 2) as g:
                    for s in range(2):
                        n = 2 * g + s
                        wait_alone(sp, p_ready, R_SLOTS + CSUB * (n - 1))
                        load_mask(n // CHUNKS, n & (CHUNKS - 1), s)

                sp.wait_ge(y_ready, IB)
                sp.dma_start(out_rows[IB - 1], y[:, 1, :, :]).then_inc(last_stored, 16)
                sp.wait_ge(last_stored, 16)

            @block.tensor
            def _(pe):
                def project(c, par, rows_in, rows_out):
                    pe.wait_ge(x1_ready, c + 1)
                    for t in range(IT):
                        pe.matmul(bank[par][:, bass.ts(t, D)], rows_in[:, bass.ts(t, P)], win[:, :],
                                  start=True, stop=True)
                        ins = pe.matmul(bank[2 + par][:, bass.ts(t, D)], rows_out[:, bass.ts(t, P)], wout[:, :],
                                        start=True, stop=True)
                    ins.then_inc(projected, 1)

                def turn_hn(c, par, turned=4):
                    pe.wait_ge(hn_ready, 2 + c + 1)
                    for t in range(IT):
                        ins = pe.transpose(bank[turned][:, bass.ts(t, P)], hn[:, par, bass.ts(t, P)], ident[:, :])
                    ins.then_inc(hn_turned, 1)

                def attend_inputs(c, par, saved, first=5):
                    pe.wait_ge(hn_t_ready, c + 1)
                    pe.wait_ge(h_saved, 1 + saved)
                    pe.matmul(bank[first][:, 0:ROWS], wa1[:, :], hn_t[:, par, :], start=True, stop=True)
                    for t in range(IT):
                        ins = pe.matmul(bank[first + 1 + t // 2][:, bass.ts(t % 2, DE)], hn_t[:, par, bass.ts(t, P)],
                                        watt[:, :], start=True, stop=True)
                    ins.then_inc(h_done, 1)

                def attend_weights():
                    pe.transpose(bank[5][:, 0:D], watt[:, 0:D], ident[:, :]).then_inc(watt_turned, 1)
                    pe.wait_ge(watt_t_ready, 1)
                    pe.wait_ge(a1wide_ready, 1)
                    pe.matmul(bank[6][:, 0:P], watt_t[:, :], a1wide[:, :], start=True, stop=True)
                    pe.matmul(bank[7][:, 0:1], watt_t[:, :], a2col[:, :], start=True, stop=True).then_inc(wa_done, 1)
                    pe.wait_ge(wa_ready, 2)

                pe.wait_ge(weights_loaded, 16 * len(weights))
                for c in range(PEELED):
                    if c == 2:
                        attend_weights()
                    rows = bass.ts(c, ROWS)
                    project(c, c % 2, in_sum[:, rows], out_sum[:, rows])
                    if c >= ATTEND_LAG:
                        attend_inputs(c - ATTEND_LAG, (c - ATTEND_LAG) % 2, c - ATTEND_LAG)
                    if c >= TURN_LAG:
                        turn_hn(c - TURN_LAG, (c - TURN_LAG) % 2)
                with pe.Fori(PEELED // 2, IB // 2) as g:
                    for par in range(2):
                        c = 2 * g + par
                        pe.wait_ge(z_loaded[par], 32 * (g - PEELED // 2 + 1))
                        project(c, par, z_in[:, par, :], z_out[:, par, :])
                        attend_inputs(c - ATTEND_LAG, (par + ATTEND_LAG) % 2, c - ATTEND_LAG)
                        turn_hn(c - TURN_LAG, (par + TURN_LAG) % 2)
                attend_inputs(IB - 5, 1, IB - 5)
                turn_hn(IB - 4, 0)
                pe.wait_ge(x1_ready, 2 + IB)
                turn_hn(IB - 3, 1, turned=0)
                attend_inputs(IB - 4, 0, IB - 4)
                turn_hn(IB - 2, 0)
                attend_inputs(IB - 3, 1, IB - 4, first=1)
                turn_hn(IB - 1, 1, turned=0)
                attend_inputs(IB - 2, 0, IB - 3)
                attend_inputs(IB - 1, 1, IB - 2, first=1)

                pe.wait_ge(top_chain, 1)
                pe.transpose(bank[0][0:1, 0:P], top_part[:, :], ident[:, :]).then_inc(top_turned, 1)
                pe.wait_ge(top_chain, 2)
                pe.matmul(bank[1][:, 0:1], ones[0:1, :], top_one[:, :], start=True, stop=True).then_inc(top_spread, 1)

                def mean_row():
                    pe.wait_ge(sum_done, IB + 1)
                    for t in range(IT):
                        ins = pe.matmul(bank[IT][:, 0:D], mean_w[:, :], h_sum[:, t, 0:D], start=(t == 0), stop=(t == IT - 1))
                    ins.then_inc(mean_done, 1)

                def chunk(b, ch, s, par, first):
                    for i in range(CSUB):
                        j = ch * CSUB + i
                        k = (s * CSUB + i) % P_SLOTS
                        pe.wait_ge(p_ready, R_SLOTS + b * SUBS + j + 1)
                        for half in range(2):
                            for t in range(IT):
                                ins = pe.matmul(bank[IT * par + t][:, 0:DE], p_tile[:, k, half, bass.ts(t, P)],
                                                hv[:, 2 * j + half, :],
                                                start=(first and i == 0 and half == 0), stop=(i == CSUB - 1 and half == 1),
                                                skip_group_check=True)
                        ins.then_inc(p_used, 1)

                def row_block(g, par, first=False):
                    b = 2 * g + par
                    pe.wait_ge(acc_free, b + 1)
                    for s in range(2):
                        pe.wait_ge(hv_ready, s + 1)
                        chunk(b, s, s, par, s == 0)
                    if first:
                        mean_row()
                    with pe.Fori(1, CHUNKS // 2) as cp:
                        for s in range(2):
                            pe.wait_ge(hv_ready, 2 * cp + s + 1)
                            chunk(b, 2 * cp + s, s, par, False)

                pe.wait_ge(top_chain, 3)
                row_block(0, 0, True)
                row_block(0, 1)
                with pe.Fori(1, IB // 2) as g:
                    for par in range(2):
                        row_block(g, par)

            @block.scalar
            def _(act):
                def normalise(g):
                    act.wait_ge(factors_ready, g + 1)
                    for t in range(LNT):
                        ins = nc.scalar.activation(hn[:, t // IT, bass.ts(t % IT, P)], x1[:, LNT * g + t, :], ACT.Relu,
                                                   bias=shift[:, t:t + 1], scale=rstd[:, t:t + 1])
                        if t % IT == IT - 1:
                            ins.then_inc(hn_ready, 1)

                def copy_turned(c, par, turned=4):
                    act.wait_ge(hn_turned, c + 1)
                    nc.scalar.copy(hn_t[:, par, :], bank[turned][:, :]).then_inc(hn_t_ready, 1)

                def save(c, first=5):
                    act.wait_ge(h_done, c + 1)
                    nc.scalar.copy(in_sum[:, bass.ts(c, ROWS)], bank[first][:, :])
                    for half in range(2):
                        ins = nc.scalar.copy(hv[:, bass.ds(c * IT + 2 * half, 2), :],
                                             bank[first + 1 + half][:, 0:2 * DE].rearrange("p (t d) -> p t d", d=DE))
                    ins.then_inc(h_saved, 1)

                act.wait_ge(watt_turned, 1)
                nc.scalar.copy(watt_t[:, :], bank[5][:, 0:D]).then_inc(watt_t_ready, 1)
                act.wait_ge(wa_done, 1)
                nc.scalar.copy(wa1[:, :], bank[6][:, 0:P]).then_inc(wa_ready, 1)
                nc.scalar.copy(watt[:, D:DE], bank[7][:, 0:1]).then_inc(wa_ready, 1)
                norm_root(act, 0, stats_ready, sqrt_done)
                normalise(0)
                norm_root(act, 1, stats_ready, sqrt_done)
                copy_turned(0, 0)
                save(0)
                copy_turned(1, 1)
                with act.Fori(PEELED // 2, IB // 2) as g:
                    for par in range(2):
                        c = 2 * g + par
                        if par == 0:
                            normalise(g - TURN_LAG // 2)
                            norm_root(act, g - 1, stats_ready, sqrt_done)
                        save(c - ATTEND_LAG)
                        copy_turned(c - TURN_LAG, par)
                normalise(IB // 2 - 2)
                norm_root(act, IB // 2 - 1, stats_ready, sqrt_done)
                save(IB - 5)
                copy_turned(IB - 4, 0)
                copy_turned(IB - 3, 1, turned=0)
                normalise(IB // 2 - 1)
                act.wait_ge(h_done, IB - 3)
                copy_turned(IB - 2, 0)
                act.wait_ge(h_done, IB - 2)
                copy_turned(IB - 1, 1, turned=0)
                nc.scalar.activation(table_probe[:, :], eps[:, :], ACT.Exp)
                act.wait_ge(h_saved, 1 + IB - 1)
                save(IB - 1, first=1)

                s2 = hv[:, :, D]
                act.wait_ge(top_chain, 3)
                nc.scalar.activation(w_col[:, :], s2, ACT.Exp, bias=w_bias[:, 0:1], scale=1 - SLOPE).then_inc(w_ready, 1)
                def c_of(b, par):
                    nc.scalar.activation(c_row[:, par, :], in_sum[:, bass.ts(b, ROWS)], ACT.Exp,
                                         bias=c_bias[:, 0:1], scale=1 - SLOPE).then_inc(c_raw, 1)

                def chunk(b, ch, s, par):
                    for i in range(CSUB):
                        j = ch * CSUB + i
                        act.wait_ge(p_ready, b * SUBS + j + 1)
                        for half in range(2):
                            ins = nc.scalar.activation(r_tile[:, i % 2, half, :], c_row[:, par, :], ACT.Relu,
                                                       bias=minus1[:, 0:1], scale=w_col[:, bass.ds(2 * j + half, 1)])
                        ins.then_inc(r_ready, 1)

                c_of(0, 0)
                nc.scalar.activation(v_col[:, :], s2, ACT.Exp, bias=v_bias[:, 0:1], scale=SLOPE).then_inc(v_ready, 1)
                act.wait_ge(w_ready, 1)
                with act.Fori(0, IB // 2) as g:
                    for par in range(2):
                        b = 2 * g + par
                        act.wait_ge(c_ready, b + 1)
                        chunk(b, 0, 0, par)
                        c_of((b + 1) & (IB - 1), 1 - par)
                        with act.Fori(1, CHUNKS) as ch:
                            chunk(b, ch, 0, par)

            @block.vector
            def _(dve):
                dve.memset(minus1[:, :], -1.0)
                dve.memset(ones[:, :], 1.0)
                dve.memset(mean_w[:, :], 1.0 / N).then_inc(consts, 1)
                dve.sem_inc(x1_ready, 2)
                dve.sem_inc(hn_ready, 2)
                dve.sem_inc(h_saved, 1)
                dve.sem_inc(y_free, 2)
                dve.sem_inc(p_ready, R_SLOTS)
                dve.sem_inc(acc_free, 1)

                dve.wait_ge(consts, 1)
                dve.wait_ge(weights_loaded, 16 * len(weights))
                dve.tensor_scalar(a1wide[:, :], ones[:, :], a1col[:, 0:1], None, ALU.mult).then_inc(a1wide_ready, 1)

                dve.tensor_reduce(degree[:, 0, :], row_parts[:, :, :], AX_X, ALU.add)
                dve.tensor_reduce(degree[:, 1, :], col_parts[:, :, :], AX_X, ALU.add).then_inc(deg_chain, 1)
                dve.wait_ge(deg_chain, 1)
                dve.tensor_scalar(positive[:, :, :], degree[:, :, :], 0.0, None, ALU.is_gt).then_inc(deg_chain, 1)
                dve.wait_ge(deg_chain, 2)
                dve.tensor_tensor(guarded[:, :, :], degree[:, :, :], positive[:, :, :], ALU.mult).then_inc(deg_chain, 1)
                dve.wait_ge(deg_chain, 3)
                dve.scalar_tensor_tensor(out=guarded[:, :, :].rearrange("p a b -> p (a b)"),
                                         in0=guarded[:, :, :].rearrange("p a b -> p (a b)"), scalar=1.0,
                                         in1=positive[:, :, :].rearrange("p a b -> p (a b)"),
                                         op0=ALU.add, op1=ALU.subtract).then_inc(deg_chain, 1)
                dve.wait_ge(deg_chain, 4)
                dve.reciprocal(inverse[:, :, :], guarded[:, :, :]).then_inc(deg_chain, 1)
                dve.wait_ge(deg_chain, 5)

                def add_share(c, par, direction):
                    for t in range(IT):
                        if direction == 1:
                            dve.wait_ge(x1_part, IT * c + t + 1)
                        row = x1[:, c * IT + t, :]
                        ins = dve.scalar_tensor_tensor(out=row, in0=bank[2 * direction + par][:, bass.ts(t, D)],
                                                       scalar=inverse[:, direction, bass.ds(c * IT + t, 1)], in1=row,
                                                       op0=ALU.mult, op1=ALU.add)
                        if direction == 0:
                            ins.then_inc(x1_part, 1)
                    if direction == 1:
                        ins.then_inc(x1_ready, 1)

                def residual(g, par):
                    dve.wait_ge(projected, 2 * g + par + 1)
                    add_share(2 * g + par, par, 0)
                    add_share(2 * g + par, par, 1)

                def moments_of(g):
                    norm_stats(dve, lambda t: x1[:, 2 * g * IT + t, :], stats_chain, STATS_CHAIN * g, stats_ready,
                               lambda par: wait_alone(dve, x1_ready, 2 + 2 * g + par + 1))

                def factors(g, first=False):
                    if not first:
                        dve.wait_ge(hn_ready, 2 + 2 * g)
                    dve.wait_ge(sqrt_done, g + 1)
                    norm_factors(dve, factors_chain, FACTORS_CHAIN * g, factors_ready)

                def two_chunks(g, second=False):
                    residual(g, 0)
                    factors(g - 1, second)
                    residual(g, 1)
                    moments_of(g)

                dve.wait_ge(x_loaded[0], 16)
                residual(0, 0)
                residual(0, 1)
                moments_of(0)
                for g in range(1, PEELED // 2):
                    dve.wait_ge(x_loaded[g], 16)
                    two_chunks(g, g == 1)
                for c in range(PEELED // 2, CB):
                    dve.wait_ge(x_loaded[c], 16)
                with dve.Fori(PEELED // 2, IB // 2) as g:
                    two_chunks(g)
                factors(IB // 2 - 1)

                for c, first in ((IB - 4, 5), (IB - 3, 1), (IB - 2, 5)):
                    dve.wait_ge(h_done, c + 1)
                    dve.tensor_copy(in_sum[:, bass.ts(c, ROWS)], bank[first][:, :])
                    for half in range(2):
                        ins = dve.tensor_copy(hv[:, c * IT + 2 * half:c * IT + 2 * half + 2, :],
                                              bank[first + 1 + half][:, 0:2 * DE].rearrange("p (t d) -> p t d", d=DE))
                    ins.then_inc(h_saved, 1)

                dve.wait_ge(h_saved, 1 + IB)
                dve.tensor_reduce(top_part[:, :], hv[:, :, D], AX_X, ALU.max).then_inc(top_chain, 1)
                dve.wait_ge(top_turned, 1)
                dve.tensor_reduce(top_one[:, :], bank[0][0:1, 0:P], AX_X, ALU.max).then_inc(top_chain, 1)
                dve.wait_ge(top_spread, 1)
                top = bank[1][:, 0:1]
                dve.tensor_scalar(w_bias[:, :], top, SLOPE - 1, None, ALU.mult)
                dve.tensor_scalar(v_bias[:, :], top, -SLOPE, None, ALU.mult)
                dve.tensor_scalar(c_bias[:, :], top, bias[:, 0:1], 1 - SLOPE, ALU.add, ALU.mult).then_inc(top_chain, 1)

                def cap(b, par):
                    dve.wait_ge(c_raw, b + 1)
                    dve.tensor_scalar(c_row[:, par, :], c_row[:, par, :], CAP, None, ALU.min).then_inc(c_ready, 1)

                def chunk(b, ch, s):
                    for i in range(CSUB):
                        q = b * SUBS + ch * CSUB + i
                        k = (s * CSUB + i) % P_SLOTS
                        dve.wait_ge(r_ready, q + 1)
                        dve.wait_ge(p_used, q + 1)
                        dve.scalar_tensor_tensor(out=p_tile[:, k, :, :].rearrange("p a b -> p (a b)"),
                                                 in0=r_tile[:, i % 2, :, :].rearrange("p a b -> p (a b)"), scalar=1.0,
                                                 in1=mask[:, s, 2 * i:2 * i + 2, :].rearrange("p a b -> p (a b)"),
                                                 op0=ALU.add, op1=ALU.mult).then_inc(p_ready, 1)

                EVAC = 3

                def finish(b, par):
                    dve.wait_ge(p_used, P_SLOTS + SUBS * (b + 1))
                    for t in range(IT):
                        ins = dve.tensor_scalar(empty[:, t:t + 1], bank[IT * par + t][:, D:DE], 0.0, None, ALU.is_equal)
                    ins.then_inc(evac_chain, 1)
                    dve.wait_ge(evac_chain, EVAC * b + 1)
                    for t in range(IT):
                        ins = dve.tensor_tensor(denom[:, t:t + 1], bank[IT * par + t][:, D:DE], empty[:, t:t + 1], ALU.add)
                    ins.then_inc(evac_chain, 1)
                    dve.wait_ge(evac_chain, EVAC * b + 2)
                    dve.reciprocal(invden[:, :], denom[:, :]).then_inc(evac_chain, 1)
                    dve.wait_ge(evac_chain, EVAC * b + 3)
                    dve.wait_ge(y_free, b + 1)
                    for t in range(IT):
                        ins = dve.scalar_tensor_tensor(out=y[:, par, t, :], in0=bank[IT * par + t][:, 0:D],
                                                       scalar=invden[:, t:t + 1], in1=x1[:, b * IT + t, :],
                                                       op0=ALU.mult, op1=ALU.add)
                    ins.then_inc(acc_free, 1)
                    dve.wait_ge(acc_free, 2 + b + 1)
                    for t in range(IT):
                        ins = dve.scalar_tensor_tensor(out=y[:, par, t, :], in0=h_mean[:, :], scalar=empty[:, t:t + 1],
                                                       in1=y[:, par, t, :], op0=ALU.mult, op1=ALU.add)
                    ins.then_inc(y_ready, 1)

                def row_block(g, par, first):
                    b = 2 * g + par
                    for s in range(2):
                        dve.wait_ge(m_loaded[s], 16 * (b * CHUNKS // 2 + 1))
                        chunk(b, s, s)
                    cap(b + 1, 1 - par)
                    if not first:
                        finish(b - 1, 1 - par)
                    with dve.Fori(1, CHUNKS // 2) as cp:
                        for s in range(2):
                            dve.wait_ge(m_loaded[s], 16 * (b * CHUNKS // 2 + cp + 1))
                            chunk(b, 2 * cp + s, s)

                cap(0, 0)
                row_block(0, 0, True)
                dve.wait_ge(mean_done, 1)
                dve.tensor_copy(h_mean[:, :], bank[IT][:, 0:D]).then_inc(acc_free, 1)
                row_block(0, 1, False)
                with dve.Fori(1, IB // 2) as g:
                    for par in range(2):
                        row_block(g, par, False)
                finish(IB - 1, 1)

            @block.gpsimd
            def _(pool):
                pool.sem_inc(p_used, P_SLOTS)
                nc.gpsimd.memset(h_sum[:, :, :], 0.0).then_inc(sum_done, 1)

                def add_h(c):
                    pool.wait_ge(h_saved, 1 + c + 1)
                    wait_alone(pool, sum_done, c + 1)
                    nc.gpsimd.tensor_tensor(h_sum[:, :, :], h_sum[:, :, :], hv[:, bass.ds(c * IT, IT), :],
                                            ALU.add).then_inc(sum_done, 1)

                with pool.Fori(0, IB - 1) as c:
                    add_h(c)

                pool.wait_ge(v_ready, 1)
                for ch in range(CHUNKS):
                    if ch == 1:
                        add_h(IB - 1)
                    if ch == CHUNKS - 1:
                        pool.wait_ge(sum_done, IB + 1)
                    at = slice(ch * CH, ch * CH + CH)
                    v = v_col[:, at].rearrange("p (t o) -> p t o", o=1)
                    nc.gpsimd.tensor_tensor(hv[:, at, 0:D], hv[:, at, 0:D], v.broadcast_to([P, CH, D]), ALU.mult)
                    nc.gpsimd.tensor_copy(hv[:, at, D:DE], v).then_inc(hv_ready, 1)

                def store(g, par):
                    b = 2 * g + par
                    pool.wait_ge(y_ready, b + 1)
                    pool.dma_start(out_rows[b], y[:, par, :, :]).then_inc(y_stored[par], 16)
                    pool.wait_ge(y_stored[par], 16 * (g + 1))
                    pool.sem_inc(y_free, 1)

                with pool.Fori(0, IB // 2 - 1) as g:
                    for par in range(2):
                        store(g, par)
                store(IB // 2 - 1, 0)


_INS = ["x", "adj", "L0_gnn_W_in", "L0_gnn_W_out", "L1_gnn_W", "L1_gnn_a1", "L1_gnn_a2", "L1_gnn_a_bias"]


def kernel(**inputs):
    import numpy as _np
    import concourse.bacc as _bacc
    from concourse import mybir as _mybir
    from concourse.bass_utils import run_bass_kernel_spmd as _run

    nc = _bacc.Bacc("TRN2", target_bir_lowering=False, num_devices=1)
    arrays, args = {}, []
    for name in _INS:
        a = _np.ascontiguousarray(inputs[name])
        arrays[f"in_{name}_dram"] = a
        args.append(nc.dram_tensor(f"in_{name}_dram", a.shape, _mybir.dt.from_np(a.dtype), kind="ExternalInput").ap())
    out = nc.dram_tensor("out_0_dram", inputs["x"].shape, _mybir.dt.float32, kind="ExternalOutput").ap()
    graph_layers(nc, *args, out)
    r = _run(nc, [arrays], core_ids=[0])
    return r.results[0]["out_0_dram"]
```
